# Optimizing a Trainium2 kernel written in Bass

```python
import numpy as np
import jax
import jax.numpy as jnp

def _softmax(x, axis=-1):
    return jax.nn.softmax(x, axis=axis)

def _gelu(x):
    return jax.nn.gelu(x, approximate=True)

def _silu(x):
    return jax.nn.silu(x)

def _sigmoid(x):
    return jax.nn.sigmoid(x)

def _layernorm(x, axis=-1, eps=1e-05):
    m = jnp.mean(x, axis=axis, keepdims=True)
    v = jnp.var(x, axis=axis, keepdims=True)
    return (x - m) / jnp.sqrt(v + eps)

def _scatter_add(tgt, idx, src, axis=0):
    return tgt.at[idx].add(src)

def _segment_sum(src, seg, n):
    return jax.ops.segment_sum(src, seg, n)
kernel_name = 'mk_prb_d1_jaxref_r8_34d001'

def setup_inputs(seed: int=0):
    np.random.seed(seed)
    _w = jnp.asarray

    def _L0_attn_setup():
        import jax, jax.numpy as jnp
        import numpy as np
        B, T, D = (1, 256, 512)
        H, G = (32, 8)
        HD = D // H
        REP = H // G
        KV_DIM = 2 * HD * G
        key = jax.random.key(seed)
        k0, k1, k2, k3 = jax.random.split(key, 4)
        x = jax.random.normal(k0, (B, T, D), dtype=jnp.float32)
        Wq = jax.random.normal(k1, (D, D), dtype=jnp.float32) * 0.02
        Wkv = jax.random.normal(k2, (D, KV_DIM), dtype=jnp.float32) * 0.02
        Wo = jax.random.normal(k3, (D, D), dtype=jnp.float32) * 0.02
        bo = jnp.zeros((D,), dtype=jnp.float32)
        return {'x': x, 'Wq': Wq, 'Wkv': Wkv, 'Wo': Wo, 'bo': bo}
    _L0_attn_in = _L0_attn_setup()

    def _L0_ffn_setup():
        import jax, jax.numpy as jnp
        import numpy as np
        H = 512
        I = 256
        E = 16
        TOPK = 4
        SI = 256
        key = jax.random.key(seed)
        ks = jax.random.split(key, 9)
        s = 0.02
        return {'hidden_states': jax.random.normal(ks[0], (2, 256, H), dtype=jnp.float32), 'gate_w': jax.random.normal(ks[1], (E, H), dtype=jnp.float32) * s, 'bias': jnp.zeros((E,), dtype=jnp.float32), 'Wg': jax.random.normal(ks[2], (E, I, H), dtype=jnp.float32) * s, 'Wu': jax.random.normal(ks[3], (E, I, H), dtype=jnp.float32) * s, 'Wd': jax.random.normal(ks[4], (E, H, I), dtype=jnp.float32) * s, 'Sg': jax.random.normal(ks[5], (SI, H), dtype=jnp.float32) * s, 'Su': jax.random.normal(ks[6], (SI, H), dtype=jnp.float32) * s, 'Sd': jax.random.normal(ks[7], (H, SI), dtype=jnp.float32) * s}
    _L0_ffn_in = _L0_ffn_setup()
    _d = {'L0_attn_x': _L0_attn_in['x'], 'L0_attn_Wq': _L0_attn_in['Wq'], 'L0_attn_Wkv': _L0_attn_in['Wkv'], 'L0_attn_Wo': _L0_attn_in['Wo'], 'L0_attn_bo': _L0_attn_in['bo'], 'L0_ffn_gate_w': _L0_ffn_in['gate_w'], 'L0_ffn_bias': _L0_ffn_in['bias'], 'L0_ffn_Wg': _L0_ffn_in['Wg'], 'L0_ffn_Wu': _L0_ffn_in['Wu'], 'L0_ffn_Wd': _L0_ffn_in['Wd'], 'L0_ffn_Sg': _L0_ffn_in['Sg'], 'L0_ffn_Su': _L0_ffn_in['Su'], 'L0_ffn_Sd': _L0_ffn_in['Sd']}
    _x0 = _d['L0_attn_x']
    _d['L0_attn_x'] = jax.random.normal(jax.random.fold_in(jax.random.key(seed), 1), (4, 256, 512), dtype=_x0.dtype)
    del _x0
    return _d

def reference(L0_attn_x, L0_attn_Wq, L0_attn_Wkv, L0_attn_Wo, L0_attn_bo, L0_ffn_gate_w, L0_ffn_bias, L0_ffn_Wg, L0_ffn_Wu, L0_ffn_Wd, L0_ffn_Sg, L0_ffn_Su, L0_ffn_Sd):

    def _L0_attn_ref(x, Wq, Wkv, Wo, bo):
        import jax, jax.numpy as jnp
        import numpy as np
        B, T, D = (1, 256, 512)
        H, G = (32, 8)
        HD = D // H
        REP = H // G
        KV_DIM = 2 * HD * G
        b, t, d = x.shape
        q = jnp.dot(x, Wq).reshape(b, t, H, HD).transpose(0, 2, 1, 3)
        kv = jnp.dot(x, Wkv).reshape(b, t, G, 2, HD).transpose(2, 3, 0, 1, 4)
        k, v = (kv[:, 0], kv[:, 1])
        k = jnp.broadcast_to(k[:, :, None], (G, b, REP, t, HD)).reshape(b, H, t, HD)
        v = jnp.broadcast_to(v[:, :, None], (G, b, REP, t, HD)).reshape(b, H, t, HD)
        scores = jnp.einsum('bhqd,bhkd->bhqk', q, k)
        causal = jnp.triu(jnp.ones((t, t), dtype=bool), 1)
        scores = jnp.where(causal[None, None], -jnp.inf, scores)
        weights = jax.nn.softmax(scores * (1.0 / HD ** 0.5), axis=-1)
        ctx = jnp.einsum('bhqk,bhkd->bhqd', weights, v)
        ctx = ctx.transpose(0, 2, 1, 3).reshape(b, t, d)
        return jnp.dot(ctx, Wo) + bo

    def _L0_ffn_ref(hidden_states, gate_w, bias, Wg, Wu, Wd, Sg, Su, Sd):
        import jax, jax.numpy as jnp
        import numpy as np
        H = 512
        I = 256
        E = 16
        TOPK = 4
        SI = 256
        orig_shape = hidden_states.shape
        x = hidden_states.reshape(-1, orig_shape[-1])
        scores = jax.nn.sigmoid(x @ gate_w.T) + bias
        topk_w, topk_idx = jax.lax.top_k(scores, TOPK)
        topk_w = topk_w / (jnp.sum(topk_w, axis=-1, keepdims=True) + 1e-20)
        cw = jnp.sum(jax.nn.one_hot(topk_idx, E, dtype=x.dtype) * topk_w[..., None], axis=1)
        g = jnp.einsum('th,eih->eti', x, Wg)
        u = jnp.einsum('th,eih->eti', x, Wu)
        z = jax.nn.silu(g) * u
        zw = z * cw.T[:, :, None]
        out = jnp.einsum('eti,ehi->th', zw, Wd)
        out = out + jax.nn.silu(x @ Sg.T) * (x @ Su.T) @ Sd.T
        return out.reshape(orig_shape)
    x = L0_attn_x
    xn = _layernorm(x, axis=-1)
    x = x + _L0_attn_ref(xn, L0_attn_Wq, L0_attn_Wkv, L0_attn_Wo, L0_attn_bo) + _L0_ffn_ref(xn, L0_ffn_gate_w, L0_ffn_bias, L0_ffn_Wg, L0_ffn_Wu, L0_ffn_Wd, L0_ffn_Sg, L0_ffn_Su, L0_ffn_Sd)
    return x

_drawn_inputs = setup_inputs


def setup_inputs(seed=0):
    import zlib

    import numpy as np

    out = dict(_drawn_inputs(seed))
    spreads = {'L0_attn_bo': (0.0, 0.1), 'L0_ffn_bias': (0.0, 0.53)}
    factors = {'L0_attn_Wq': 8.0,
     'L0_ffn_gate_w': 4.329,
     'L0_ffn_Wg': 3.313,
     'L0_ffn_Wu': 3.262,
     'L0_ffn_Wd': 3.241}
    for name, (base, spread) in spreads.items():
        noise = np.random.default_rng([zlib.crc32(name.encode()), seed]).standard_normal(out[name].shape)
        drawn = base * np.exp(spread * noise) if base else spread * noise
        out[name] = jnp.asarray(drawn.astype(out[name].dtype))
    for name, factor in factors.items():
        out[name] = (out[name] * factor).astype(out[name].dtype)
    return out
```

```python
from contextlib import ExitStack

import concourse.bass as bass
from concourse import mybir

F32 = mybir.dt.float32
F32R = mybir.dt.float32r
BF16 = mybir.dt.bfloat16
F16 = mybir.dt.float16
I32 = mybir.dt.int32
ALU = mybir.AluOpType
ACT = mybir.ActivationFunctionType
AX = mybir.AxisListType

P = 128
B, T, D = 4, 256, 512
NTOK = B * T
NT = NTOK // P
KD = D // P
H, G = 32, 8
HD = D // H
REP = H // G
QT = T // P
NE, TOPK, FI = 16, 4, 256
FK = FI // P
NSLOT = (TOPK * NTOK + (NE - TOPK) + NE * (P - 1)) // P
NBUF = 3
WCOLS = KD * 2 * FI + FK * D
GUC = KD * 2 * FI
VG = G * HD + NE
QROWS = 3 * HD
VCOL = 3 * HD + 1
QF = H * HD // P
SCALE = HD ** -0.5
BIG = 1.0e30
EPS = 1e-5


class Steps:

    def __init__(self, eng, sem):
        self.eng, self.sem, self.base, self.n = eng, sem, 0, 0

    def did(self, instruction):
        instruction.then_inc(self.sem, 1)
        self.n += 1

    def wait(self):
        self.eng.wait_ge(self.sem, self.base + self.n)


def block_program(nc, x, wqk, wvg, wo, bo, ebias, wexp, out):
    table = nc.dram_tensor("slot_table", [P, NSLOT * 2], F32, kind="Internal").ap()
    xn_rows = nc.dram_tensor("xn_rows", [NTOK, D], F32, kind="Internal").ap()
    q_parts = nc.dram_tensor("q_parts", [QF, P, 2, T], F32, kind="Internal").ap()
    k_parts = nc.dram_tensor("k_parts", [P, 2, NTOK], F32, kind="Internal").ap()
    y_rows = nc.dram_tensor("y_rows", [NSLOT * P, D], F32, kind="Internal").ap()

    ctx = ExitStack()
    with ctx:
        def sb(name, shape, dt):
            return ctx.enter_context(nc.sbuf_tensor(name, shape, dt))

        def sem(name):
            return ctx.enter_context(nc.semaphore(name))

        acc = sb("acc", [P, NT, D], F32)
        xn = sb("xn", [P, NT, D], F32)
        xT = sb("xT", [P, KD, NTOK], F32)
        wbuf = sb("wbuf", [P, NBUF, WCOLS], F32)
        wqk_sb = sb("wqk_sb", [P, KD, (H + G) * HD], F32)
        wvg_sb = sb("wvg_sb", [P, KD, VG], F32)
        wo_sb = sb("wo_sb", [P, KD, D], F32)
        bo_sb = sb("bo_sb", [P, D], F32)
        ebias_sb = sb("ebias_sb", [P, NE], F32)
        stage = sb("stage", [P, 2, QF, T], F32R)
        q_pack = sb("q_pack", [P, H // 2, T], F32R)
        k_pack = sb("k_pack", [P, B, T], F32R)
        v_pack = sb("v_pack", [P, NT, G, VCOL + 1], BF16)
        ident = sb("ident", [P, P], F32)
        ident_b = sb("ident_b", [P, P], BF16)
        mask_b = sb("mask_b", [P, P], BF16)
        before_b = sb("before_b", [P, P], BF16)
        ones_b = sb("ones_b", [P, P], BF16)
        ones_f = sb("ones_f", [P, NT * NE], F32)
        kcount = sb("kcount", [P, TOPK], F32)
        tile4 = sb("tile4", [P, NT], F32)
        lim = sb("lim", [P, NT - 1], F32)
        siota = sb("siota", [P, NSLOT], F32)
        zeros = sb("zeros", [P, NSLOT * 2], F32)
        gidx = sb("gidx", [P, 2], I32)
        gnone = sb("gnone", [P, 2], F32)
        xg = sb("xg", [P, 2, D], F32)
        xgT = sb("xgT", [P, 2, KD, P], F32)
        th = sb("th", [P, 2, FI], F32)
        zh = sb("zh", [P, FI], F32)
        zz = sb("zz", [P, 2, FI], F32)
        zT = sb("zT", [P, 2, FK, P], F32)
        ysb = sb("ysb", [P, 2, D], F32)
        pexp = wbuf[:, 0, 0:3072].rearrange("p (b n) -> p b n", b=2)
        phi = wbuf[:, 1, 0:1536].bitcast(F16).rearrange("p (b n) -> p b n", b=2)
        plo = wbuf[:, 2, 0:1536].bitcast(F16).rearrange("p (b n) -> p b n", b=2)
        negm = sb("negm", [P, 2 * QT, H], F32)
        negmT = sb("negmT", [QT * H, P], F32R)
        den = sb("den", [P, QT * REP], F32)
        csum = sb("csum", [P, QT * REP, HD], F32)
        ctxs = sb("ctxs", [P, QT, D], F32)
        ctxT = sb("ctxT", [P, QT, KD, P], F32)
        osb = ysb
        stats = sb("stats", [P, NT, 6], F32)
        mv = sb("mv", [P, NT, 2], F32)
        sm = sb("sm", [P, 7, NT], F32)
        vg_sb = sb("vg_sb", [P, NT, VG], F32)
        vres = sb("vres", [P, 2, NT, G * HD], F32)
        rt = sb("rt", [P, 14, NT, NE], F32)
        top8 = sb("top8", [P, NT, 8], F32)
        need = sb("need", [P, 6, NT], F32)
        mask16 = sb("mask16", [P, NT, NE], BF16)
        oh = sb("oh", [P, 4, NT, TOPK, NE], F32)
        ecount = sb("ecount", [P, 6, NE], F32)
        sgt = sb("sgt", [P, NE, NT - 1], F32)
        scmp = oh[:, 2:4].rearrange("p c t k e -> p (c t k e)")[:, 0:NSLOT * NE].rearrange("p (s e) -> p s e", e=NE)
        sexp = sb("sexp", [P, 2, NSLOT], F32)
        sexp_i = sb("sexp_i", [P, 5, NSLOT], I32)
        end_i = sb("end_i", [P, NE], I32)
        dest_f = sb("dest_f", [P, NT, TOPK], F32)
        dest_i = sb("dest_i", [P, NT, TOPK], I32)
        tpos_i = sb("tpos_i", [P, 4, NT, TOPK], I32)
        pair = sb("pair", [P, NT, TOPK, 2], F32)
        tab = sb("tab", [P, NSLOT, 2], F32)

        psum = ctx.enter_context(nc.psum_tensor("psum", [P, 8, 512], F32))

        def bank(i, cols=512):
            return psum[:, i, 0:cols]

        (const_ready, credit, sqrt_in, sqrt_done, dve_step, dve2, pool_step, xn_ready, xnT_ps, xnT_sb, xn_stored,
         vg_ps, vg_done, rexp_done, mask_ready, ranks_ps, slots_known, pair_ready, table_zero, scattered,
         table_back, bo_added, v_ready) = [sem(n) for n in (
            "const_ready credit sqrt_in sqrt_done dve_step dve2 pool_step xn_ready xnT_ps xnT_sb xn_stored "
            "vg_ps vg_done rexp_done mask_ready ranks_ps slots_known pair_ready table_zero scattered "
            "table_back bo_added v_ready").split()]
        (xt_ps, xt_sb, gu_ps, th_done, z_done, zt_ps, zt_sb, dn_ps, y_sb) = [sem(n) for n in (
            "xt_ps xt_sb gu_ps th_done z_done zt_ps zt_sb dn_ps y_sb").split()]
        (qk_ps, hi_done, lo_done, packed, ones_set, max_ps, negm_done, nmT_ps, nmT_sb, nm_in, st_ps, exp_done,
         masked, hi16_done, lo16_done, pv_ps, csum_done, ctx_done, ct_ps, ct_sb, wo_ps, out_sb) = [sem(n) for n in (
            "qk_ps hi_done lo_done packed ones_set max_ps negm_done nmT_ps nmT_sb nm_in st_ps exp_done "
            "masked hi16_done lo16_done pv_ps csum_done ctx_done ct_ps ct_sb wo_ps out_sb").split()]
        x_in = [sem(f"x_in{i}") for i in range(4)]
        wvg_in, wqk_in, wo_in, small_in = sem("wvg_in"), sem("wqk_in"), sem("wo_in"), sem("small_in")
        we_in = [sem(f"we_in{i}") for i in range(NBUF)]
        xg_in = [sem(f"xg_in{i}") for i in range(2)]
        y_out = [sem(f"y_out{i}") for i in range(2)]
        k_out = sem("k_out")
        parts_out = [sem(f"parts_out{i}") for i in range(QF)]
        comb = [sem(f"comb{i}") for i in range(TOPK)]
        out_dma = [sem(f"out_dma{i}") for i in range(QT)]

        w_ready, sh_sb = sem("w_ready"), sem("sh_sb")

        def arrivals(e):
            return e // NBUF + 1 + (e % NBUF == NBUF - 1)

        PACKS = 18 * 16
        U0 = NT
        NU = NT + NSLOT

        block = ctx.enter_context(nc.Block())

        @block.sync
        def _(sp):
            for i in range(4):
                sp.dma_start(acc[:, 2 * i:2 * i + 2, :],
                             x[2 * i * P:(2 * i + 2) * P, :].rearrange("(t p) d -> p t d", p=P)).then_inc(x_in[i], 16)
            sp.dma_start(wvg_sb[:, :, :], wvg).then_inc(wvg_in, 16)
            sp.dma_start(ebias_sb[:, :], ebias.rearrange("(a n) -> a n", a=1).broadcast_to([P, NE])).then_inc(small_in, 16)
            sp.dma_start(bo_sb[:, :], bo.rearrange("(a n) -> a n", a=1).broadcast_to([P, D])).then_inc(small_in, 16)
            sp.dma_start(wbuf[:, NBUF - 1, :], wexp[NE]).then_inc(we_in[NBUF - 1], 16)
            sp.dma_start(wqk_sb[:, :, :], wqk).then_inc(wqk_in, 16)
            for t in range(NT):
                sp.wait_ge(xn_ready, t + 1)
                sp.dma_start(xn_rows[t * P:(t + 1) * P, :], xn[:, t, :]).then_inc(xn_stored, 16)
            for e in range(NBUF - 1):
                sp.dma_start(wbuf[:, e, :], wexp[e]).then_inc(we_in[e], 16)
            sp.dma_start(wo_sb[:, :, :], wo).then_inc(wo_in, 16)
            sp.wait_ge(scattered, 16 * NT * TOPK)
            sp.dma_start(tab[:, :, :].rearrange("p s c -> p (s c)"), table).then_inc(table_back, 16)
            sp.wait_ge(slots_known, 1)
            for e in range(NBUF - 1, NE):
                sp.wait_ge(we_in[(e - 2) % NBUF], 16 * arrivals(e - 2))
                sp.sem_inc(w_ready, 1)
                if e == NBUF - 1:
                    sp.wait_ge(dn_ps, U0)
                else:
                    last = sp.value_load(end_i[0:1, e - NBUF:e - NBUF + 1], min_val=1, max_val=NSLOT)
                    sp.wait_ge(dn_ps, last + U0)
                sp.dma_start(wbuf[:, e % NBUF, :], wexp[e]).then_inc(we_in[e % NBUF], 16)
            for e in (NE - 2, NE - 1):
                sp.wait_ge(we_in[e % NBUF], 16 * arrivals(e))
                sp.sem_inc(w_ready, 1)
            for c in range(B):
                sp.wait_ge(lo_done, c + 3)
                sp.dma_start(k_parts[:, :, c * T:(c + 1) * T], stage[:, :, c, :].bitcast(F32)).then_inc(k_out, 16)
            sp.wait_ge(k_out, 16 * B)
            sp.wait_ge(ones_set, 1)
            with sp.Fori(0, B) as b:
                sp.wait_ge(st_ps, G * b + 1)
                for row, part in enumerate((0, 1, 0)):
                    for half in range(2):
                        base = 64 * half + HD * row
                        sp.dma_start(k_pack[base:base + HD, :, :].rearrange("r c t -> r (c t)").bitcast(F32),
                                     k_parts[bass.ds(2 * HD * b + half * HD, HD), part, :]).then_inc(packed, 16)
                for f in range(QF):
                    sp.wait_ge(lo_done, QF * b + (B + f + 3))
                    sp.dma_start(q_parts[f], stage[:, :, f, :].bitcast(F32)).then_inc(parts_out[f], 16)
                for f in range(QF):
                    sp.wait_ge(parts_out[f], 16 * b + 16)
                    for row, part in enumerate((0, 0, 1)):
                        base = 64 * (f // 2) + HD * row
                        sp.dma_start(q_pack[base:base + HD, 8 * (f % 2):8 * (f % 2) + 8, :].bitcast(F32),
                                     q_parts[f, :, part, :].rearrange("(h r) t -> r h t", r=HD)).then_inc(packed, 16)
                sp.wait_ge(nmT_sb, b + 1)
                for qt in range(QT):
                    for half in range(2):
                        sp.dma_start(q_pack[64 * half + QROWS:64 * half + QROWS + 1, :, qt * P:(qt + 1) * P].bitcast(F32),
                                     negmT[qt * H + 16 * half:qt * H + 16 * half + 16, :].bitcast(F32)).then_inc(nm_in, 16)
                for qt in range(QT):
                    sp.wait_ge(out_sb, 2 * b + qt + 2)
                    sp.dma_start(out[bass.ds((2 * b + qt) * P, P), :], osb[:, qt, :]).then_inc(out_dma[qt], 16)
            for qt in range(QT):
                sp.wait_ge(out_dma[qt], 16 * B + 1)

        @block.gpsimd
        def _(pool):
            own = Steps(pool, pool_step)
            pool.sem_inc(exp_done, 1)
            own.did(nc.gpsimd.memset(ident[:, :], 0.0))
            own.did(nc.gpsimd.memset(ident_b[:, :], 0.0))
            own.did(nc.gpsimd.memset(mask_b[:, :], 0.0))
            own.did(nc.gpsimd.memset(before_b[:, :], 1.0))
            own.did(nc.gpsimd.memset(zeros[:, :], 0.0))
            own.did(nc.gpsimd.memset(ones_b[:, :], 1.0))
            own.did(nc.gpsimd.memset(ones_f[:, :], 1.0))
            own.did(nc.gpsimd.memset(v_pack[:, :, :, :], 1.0))
            own.wait()
            for m in (ident, ident_b):
                own.did(nc.gpsimd.affine_select(out=m[:, :], in_=m[:, :], compare_op=ALU.not_equal, fill=1.0, base=0,
                                                pattern=[[-1, P]], channel_multiplier=1))
            own.did(nc.gpsimd.affine_select(out=mask_b[:, :], in_=mask_b[:, :], compare_op=ALU.is_ge, fill=-BIG, base=0,
                                            pattern=[[-1, P]], channel_multiplier=1))
            own.did(nc.gpsimd.affine_select(out=before_b[:, :], in_=before_b[:, :], compare_op=ALU.is_gt, fill=0.0, base=0,
                                            pattern=[[1, P]], channel_multiplier=-1))
            for m, step, base in ((kcount, 1, 1), (tile4, TOPK, 0), (lim, P, P), (siota, 1, 0)):
                own.did(nc.gpsimd.iota(m[:, :], pattern=[[step, m.shape[1]]], base=base, channel_multiplier=0,
                                       allow_small_or_imprecise_dtypes=True))
            for k in range(TOPK):
                own.did(nc.gpsimd.iota(pair[:, :, k, 0].bitcast(I32), pattern=[[P, NT]], base=0, channel_multiplier=1))
            own.wait()
            pool.dma_start(table, zeros[:, :]).then_inc(table_zero, 16)
            pool.sem_inc(const_ready, 1)
            pool.wait_ge(xn_ready, NT)
            pool.wait_ge(small_in, 32)
            nc.gpsimd.tensor_tensor(acc[:, :, :], acc[:, :, :],
                                    bo_sb[:, :].rearrange("p (a d) -> p a d", a=1).broadcast_to([P, NT, D]),
                                    ALU.add).then_inc(bo_added, 1)
            pool.wait_ge(table_zero, 16)
            pool.wait_ge(pair_ready, 1)
            for j in range(NT):
                for k in range(TOPK):
                    nc.gpsimd.indirect_dma_start(
                        out=table.rearrange("p (s c) -> (p s) c", c=2),
                        out_offset=bass.IndirectOffsetOnAxis(ap=tpos_i[:, 3, j, k:k + 1], axis=0),
                        in_=pair[:, j, k, :], in_offset=None).then_inc(scattered, 16)
            pool.wait_ge(table_back, 16)
            pool.wait_ge(xn_stored, 16 * NT)

            def gather(s, par, free):
                if free is not None:
                    pool.wait_ge(xt_ps, free)
                own.did(nc.gpsimd.tensor_copy(gidx[:, par:par + 1], tab[:, bass.ds(s, 1), 0].bitcast(I32)))
                own.wait()
                own.did(nc.gpsimd.tensor_tensor(gnone[:, par:par + 1], ones_f[:, 0:1], ones_f[:, 0:1], ALU.mult))
                nc.gpsimd.indirect_dma_start(
                    out=xg[:, par, :], out_offset=None, in_=xn_rows,
                    in_offset=bass.IndirectOffsetOnAxis(ap=gidx[:, par:par + 1], axis=0)).then_inc(xg_in[par], 16)

            gather(0, 0, None)
            gather(1, 1, None)
            n0 = own.n
            with pool.Fori(0, (NSLOT - 3) // 2) as i:
                own.base, own.n = n0 + 4 * i, 0
                gather(2 * i + 2, 0, 2 * i + 1)
                gather(2 * i + 3, 1, 2 * i + 2)
            own.base, own.n = 0, n0 + 2 * (NSLOT - 3)
            gather(NSLOT - 1, 0, NSLOT - 2)
            pool.wait_ge(y_out[0], 16 * ((NSLOT + 1) // 2))
            pool.wait_ge(y_out[1], 16 * (NSLOT // 2))
            pool.wait_ge(sh_sb, NT)
            for b in range(B):
                for g in range(G):
                    i = G * b + g
                    j, k = i // TOPK, i % TOPK
                    if k:
                        pool.wait_ge(comb[k - 1], 16 * (j + 1))
                    nc.gpsimd.indirect_dma_start(
                        out=acc[:, j, :], out_offset=None, in_=y_rows,
                        in_offset=bass.IndirectOffsetOnAxis(ap=dest_i[:, j, k:k + 1], axis=0),
                        compute_op=ALU.add).then_inc(comb[k], 16)
                    pool.wait_ge(exp_done, i + 2)
                    par = g % 2
                    first = pexp[:, par, 0:1024].rearrange("p (r q) -> p r q", r=REP)[:, :, 0:P]
                    second = pexp[:, par, 1024:1536].rearrange("p (r q) -> p r q", r=REP)
                    for m, block_ in enumerate((first, second)):
                        nc.gpsimd.affine_select(out=block_, in_=block_, compare_op=ALU.is_ge, fill=0.0, base=0,
                                                pattern=[[0, REP], [1, P]], channel_multiplier=-1).then_inc(masked, 1)

        @block.scalar
        def _(act):
            act.sem_inc(y_sb, 2)
            act.wait_ge(sqrt_in, 1)
            nc.scalar.activation(sm[:, 1, :], sm[:, 0, :], ACT.Sqrt).then_inc(sqrt_done, 1)
            for t in range(NT):
                act.wait_ge(xnT_ps, t + 1)
                nc.scalar.activation(xT[:, :, t * P:(t + 1) * P],
                                     bank(t % 2).rearrange("p (k n) -> p k n", k=KD), ACT.Copy).then_inc(xnT_sb, 1)
            for t in range(NT):
                act.wait_ge(vg_ps, t + 1)
                nc.scalar.activation(vg_sb[:, t, :], bank(2 + t % 2, VG), ACT.Copy).then_inc(vg_done, 1)
            act.wait_ge(vg_done, NT)
            nc.scalar.activation(rt[:, 0, :, :], vg_sb[:, :, G * HD:VG], ACT.Exp, scale=-1.0).then_inc(rexp_done, 1)

            def tanh(n, par):
                act.wait_ge(gu_ps, n + 1)
                act.wait_ge(z_done, n - 1)
                nc.scalar.activation(th[:, par, :], bank(4 + par, FI), ACT.Tanh, scale=0.5).then_inc(th_done, 1)

            def zt_evac(n, par):
                act.wait_ge(zt_ps, n + 1)
                nc.scalar.activation(zT[:, par, :, :], bank(3, FI).rearrange("p (k n) -> p k n", k=FK),
                                     ACT.Copy).then_inc(zt_sb, 1)

            def y_evac(n, s, par, count):
                act.wait_ge(dn_ps, n + 1)
                if count is not None:
                    act.wait_ge(y_out[par], count)
                nc.scalar.activation(ysb[:, par, :], bank(6 + par), ACT.Copy,
                                     scale=tab[:, bass.ds(s, 1), 1]).then_inc(y_sb, 1)
                act.wait_ge(y_sb, s + 3)
                act.dma_start(y_rows[bass.ds(s * P, P), :], ysb[:, par, :]).then_inc(y_out[par], 16)

            for n in range(NT):
                act.wait_ge(gu_ps, n + 1)
                if n >= 2:
                    act.wait_ge(z_done, n - 1)
                nc.scalar.activation(th[:, n % 2, :], bank(4 + n % 2, FI), ACT.Tanh, scale=0.5).then_inc(th_done, 1)
                if n:
                    zt_evac(n - 1, (n - 1) % 2)
            act.wait_ge(table_back, 16)
            tanh(U0, 0)
            zt_evac(U0 - 1, 1)
            for n in (U0 + 1, U0 + 2):
                tanh(n, n % 2)
                zt_evac(n - 1, (n - 1) % 2)
                y_evac(n - 1, n - 1 - U0, (n - 1) % 2, None)
            with act.Fori(0, (NSLOT - 3) // 2) as i:
                for q in range(2):
                    n = 2 * i + (U0 + 3 + q)
                    tanh(n, (1 + q) % 2)
                    zt_evac(n - 1, q % 2)
                    y_evac(n - 1, n - 1 - U0, q % 2, 16 * i + 16)
            zt_evac(NU - 1, 0)
            y_evac(NU - 1, NSLOT - 1, 0, 16 * ((NSLOT - 1) // 2))

            for c in range(B):
                act.wait_ge(qk_ps, c + 1)
                nc.scalar.activation(stage[:, 0, c, :], bank(c % 2, T), ACT.Copy).then_inc(hi_done, 1)
            act.wait_ge(k_out, 16 * B)
            with act.Fori(0, B) as b:
                for f in range(QF):
                    act.wait_ge(qk_ps, QF * b + (B + f + 1))
                    if f == 0:
                        act.wait_ge(packed, PACKS * b + 1)
                    nc.scalar.activation(stage[:, 0, f, :], bank(f % 2, T), ACT.Copy).then_inc(hi_done, 1)
                act.wait_ge(nmT_ps, b + 1)
                nc.scalar.activation(negmT[:, :], psum[0:QT * H, 5, 0:P], ACT.Copy).then_inc(nmT_sb, 1)

                def high(g):
                    act.wait_ge(masked, 2 * (G * b + g + 1))
                    act.wait_ge(pv_ps, G * b + g + 1)
                    nc.scalar.activation(phi[:, g % 2, :], pexp[:, g % 2, :], ACT.Copy).then_inc(hi16_done, 1)

                for g in range(G):
                    act.wait_ge(st_ps, G * b + g + 2)
                    act.wait_ge(lo16_done, G * b + g + 1)
                    nc.scalar.activation(pexp[:, g % 2, :], psum[:, 2:5, :].rearrange("p a n -> p (a n)"), ACT.Exp,
                                         scale=SCALE).then_inc(exp_done, 1)
                    if g:
                        high(g - 1)
                high(G - 1)
                for qt in range(QT):
                    act.wait_ge(ct_ps, QT * b + qt + 1)
                    nc.scalar.activation(ctxT[:, qt, :, :], bank(6 + qt).rearrange("p (k n) -> p k n", k=KD),
                                         ACT.Copy).then_inc(ct_sb, 1)

        @block.vector
        def _(dve):
            own = Steps(dve, dve_step)
            V = nc.vector
            dve.sem_inc(lo_done, 2)
            dve.sem_inc(negm_done, 2)
            dve.sem_inc(lo16_done, 2)
            dve.sem_inc(csum_done, 1)
            dve.sem_inc(out_sb, 1)
            for qt in range(QT):
                dve.sem_inc(out_dma[qt], 1)
            for t in range(NT):
                dve.wait_ge(x_in[t // 2], 16)
                own.did(V.bn_stats(stats[:, t, :], acc[:, t, :]))
            own.wait()
            for t in range(NT):
                own.did(V.bn_aggr(mv[:, t, :], stats[:, t, :]))
            own.wait()
            V.tensor_scalar(sm[:, 0, :], mv[:, :, 1], EPS, None, ALU.add).then_inc(sqrt_in, 1)
            dve.wait_ge(sqrt_done, 1)
            own.did(V.reciprocal(sm[:, 2, :], sm[:, 1, :]))
            own.wait()
            own.did(V.tensor_tensor(sm[:, 3, :], sm[:, 2, :], sm[:, 2, :], ALU.mult))
            own.wait()
            own.did(V.tensor_tensor(sm[:, 4, :], sm[:, 3, :], sm[:, 0, :], ALU.mult))
            own.wait()
            own.did(V.tensor_scalar(sm[:, 5, :], sm[:, 4, :], -0.5, 1.5, ALU.mult, ALU.add))
            own.wait()
            own.did(V.tensor_tensor(sm[:, 6, :], sm[:, 5, :], sm[:, 2, :], ALU.mult))
            own.wait()
            for t in range(NT):
                V.tensor_scalar(xn[:, t, :], acc[:, t, :], mv[:, t, 0:1], sm[:, 6, t:t + 1], ALU.subtract,
                                ALU.mult).then_inc(xn_ready, 1)

            def op(ins):
                own.did(ins)
                own.wait()

            def over_experts(a):
                return a.rearrange("p (t a) -> p t a", a=1).broadcast_to([P, NT, NE])

            dve.wait_ge(rexp_done, 1)
            dve.wait_ge(small_in, 32)
            op(V.tensor_scalar(rt[:, 1, :, :], rt[:, 0, :, :], 1.0, None, ALU.add))
            op(V.reciprocal(rt[:, 2, :, :], rt[:, 1, :, :]))
            score = rt[:, 3, :, :]
            op(V.tensor_tensor(score, rt[:, 2, :, :],
                               ebias_sb[:, :].rearrange("p (a e) -> p a e", a=1).broadcast_to([P, NT, NE]), ALU.add))
            for t in range(NT):
                own.did(V.max(top8[:, t, :], score[:, t, :]))
            own.wait()
            fourth = top8[:, :, TOPK - 1:TOPK].broadcast_to([P, NT, NE])
            above, equal = rt[:, 4, :, :], rt[:, 5, :, :]
            own.did(V.tensor_tensor(above, score, fourth, ALU.is_gt))
            op(V.tensor_tensor(equal, score, fourth, ALU.is_equal))
            own.did(V.tensor_reduce(need[:, 0, :], above, AX.X, ALU.add))
            flat = lambda a: a.rearrange("p t e -> p (t e)")
            op(V.tensor_tensor_scan(flat(rt[:, 6, :, :]), ones_f[:, :], flat(equal), 0.0, ALU.mult, ALU.add))
            own.did(V.tensor_scalar(need[:, 1, :], need[:, 0, :], -1.0, float(TOPK), ALU.mult, ALU.add))
            op(V.tensor_tensor(need[:, 2, :], rt[:, 6, :, 0], equal[:, :, 0], ALU.subtract))
            op(V.tensor_tensor(need[:, 3, :], need[:, 1, :], need[:, 2, :], ALU.add))
            op(V.tensor_tensor(rt[:, 7, :, :], rt[:, 6, :, :], over_experts(need[:, 3, :]), ALU.is_le))
            op(V.tensor_tensor(rt[:, 8, :, :], rt[:, 7, :, :], equal, ALU.mult))
            chosen = rt[:, 9, :, :]
            op(V.tensor_tensor(chosen, rt[:, 8, :, :], above, ALU.add))
            V.tensor_copy(mask16[:, :, :], chosen).then_inc(mask_ready, 1)
            own.did(V.tensor_tensor_scan(flat(rt[:, 10, :, :]), ones_f[:, :], flat(chosen), 0.0, ALU.mult, ALU.add))
            op(V.tensor_tensor(rt[:, 11, :, :], chosen, score, ALU.mult))
            own.did(V.tensor_tensor(rt[:, 12, :, :], rt[:, 10, :, :], over_experts(tile4[:, :]), ALU.subtract))
            op(V.tensor_reduce(need[:, 4, :], rt[:, 11, :, :], AX.X, ALU.add))
            op(V.tensor_scalar(need[:, 4, :], need[:, 4, :], 1e-20, None, ALU.add))
            op(V.reciprocal(need[:, 5, :], need[:, 4, :]))
            op(V.tensor_tensor(rt[:, 13, :, :], rt[:, 11, :, :], over_experts(need[:, 5, :]), ALU.mult))

            def per_choice(a):
                return a.rearrange("p t (a e) -> p t a e", a=1).broadcast_to([P, NT, TOPK, NE])

            op(V.tensor_tensor(oh[:, 0], per_choice(rt[:, 12, :, :]),
                               kcount[:, :].rearrange("p (a k c) -> p a k c", a=1, c=1).broadcast_to([P, NT, TOPK, NE]),
                               ALU.is_equal))
            op(V.tensor_tensor(oh[:, 1], oh[:, 0], per_choice(chosen), ALU.mult))
            op(V.tensor_tensor(oh[:, 2], oh[:, 1], per_choice(rt[:, 13, :, :]), ALU.mult))
            op(V.tensor_reduce(pair[:, :, :, 1], oh[:, 2], AX.X, ALU.add))
            dve.wait_ge(ranks_ps, 2)
            op(V.tensor_copy(ecount[:, 0, :], bank(1, NE)))
            by_limit = [P, NE, NT - 1]
            op(V.tensor_tensor(sgt[:, :, :], ecount[:, 0, :].rearrange("p (e a) -> p e a", a=1).broadcast_to(by_limit),
                               lim[:, :].rearrange("p (a m) -> p a m", a=1).broadcast_to(by_limit), ALU.is_gt))
            op(V.tensor_reduce(ecount[:, 1, :], sgt[:, :, :], AX.X, ALU.add))
            op(V.tensor_scalar(ecount[:, 2, :], ecount[:, 1, :], 1.0, None, ALU.add))
            op(V.tensor_tensor_scan(ecount[:, 3, :], ones_f[:, 0:NE], ecount[:, 2, :], 0.0, ALU.mult, ALU.add))
            op(V.tensor_tensor(ecount[:, 4, :], ecount[:, 3, :], ecount[:, 2, :], ALU.subtract))
            op(V.tensor_scalar(ecount[:, 5, :], ecount[:, 4, :], float(P), None, ALU.mult))
            op(V.tensor_tensor(rt[:, 1, :, :], bank(0, NT * NE).rearrange("p (t e) -> p t e", t=NT),
                               ecount[:, 5, :].rearrange("p (a e) -> p a e", a=1).broadcast_to([P, NT, NE]), ALU.add))
            op(V.tensor_tensor(oh[:, 3], oh[:, 1], per_choice(rt[:, 1, :, :]), ALU.mult))
            op(V.tensor_reduce(dest_f[:, :, :], oh[:, 3], AX.X, ALU.add))
            op(V.tensor_copy(dest_i[:, :, :], dest_f[:, :, :]))
            own.did(V.tensor_scalar(tpos_i[:, 0], dest_i[:, :, :], 7, None, ALU.arith_shift_right))
            op(V.tensor_scalar(tpos_i[:, 1], dest_i[:, :, :], P - 1, None, ALU.bitwise_and))
            op(V.tensor_scalar(tpos_i[:, 2], tpos_i[:, 1], float(NSLOT), None, ALU.mult))
            V.tensor_tensor(tpos_i[:, 3], tpos_i[:, 2], tpos_i[:, 0], ALU.add).then_inc(pair_ready, 1)
            by_slot = [P, NSLOT, NE]
            op(V.tensor_tensor(scmp[:, :, :], siota[:, :].rearrange("p (s a) -> p s a", a=1).broadcast_to(by_slot),
                               ecount[:, 3, :].rearrange("p (a e) -> p a e", a=1).broadcast_to(by_slot), ALU.is_ge))
            op(V.tensor_reduce(sexp[:, 0, :], scmp[:, :, :], AX.X, ALU.add))
            op(V.tensor_scalar(sexp[:, 1, :], sexp[:, 0, :], float(NE - 1), None, ALU.min))
            op(V.tensor_copy(sexp_i[:, 0, :], sexp[:, 1, :]))
            op(V.tensor_scalar(sexp_i[:, 1, :], sexp_i[:, 0, :], 11.0, None, ALU.mult))
            op(V.tensor_scalar(sexp_i[:, 2, :], sexp_i[:, 1, :], 5, None, ALU.arith_shift_right))
            op(V.tensor_scalar(sexp_i[:, 3, :], sexp_i[:, 2, :], -float(NBUF), None, ALU.mult))
            own.did(V.tensor_tensor(sexp_i[:, 4, :], sexp_i[:, 3, :], sexp_i[:, 0, :], ALU.add))
            op(V.tensor_copy(end_i[:, :], ecount[:, 3, :]))
            V.tensor_copy(need[:, 0, :], need[:, 1, :]).then_inc(slots_known, 1)

            n1 = own.n

            def gated(n, par):
                dve.wait_ge(th_done, n + 1)
                if not isinstance(n, int) or n:
                    dve.wait_ge(z_done, n)
                own.did(V.scalar_tensor_tensor(out=zh[:, :], in0=th[:, par, :], scalar=1.0, in1=bank(4 + par, FI),
                                               op0=ALU.add, op1=ALU.mult))
                own.wait()
                V.scalar_tensor_tensor(out=zz[:, par, :], in0=zh[:, :], scalar=0.5, in1=psum[:, 4 + par, FI:2 * FI],
                                       op0=ALU.mult, op1=ALU.mult).then_inc(z_done, 1)

            def xt_evac(s, par):
                dve.wait_ge(xt_ps, s + 1)
                V.tensor_copy(xgT[:, par, :, :], bank(2).rearrange("p (k n) -> p k n", k=KD)).then_inc(xt_sb, 1)

            def shared_out(n):
                dve.wait_ge(dn_ps, n + 1)
                dve.wait_ge(bo_added, 1)
                V.tensor_tensor(acc[:, n, :], acc[:, n, :], bank(6 + n % 2), ALU.add).then_inc(sh_sb, 1)

            def zz_free(n):
                if not isinstance(n, int) or n >= 2:
                    dve.wait_ge(zt_ps, n - 1)

            for n in range(NT):
                zz_free(n)
                gated(n, n % 2)
                if n:
                    shared_out(n - 1)
            xt_evac(0, 0)
            zz_free(U0)
            gated(U0, 0)
            shared_out(NT - 1)
            xt_evac(1, 1)
            n2 = own.n
            with dve.Fori(0, (NSLOT - 3) // 2) as i:
                own.base, own.n = n2 + 2 * i, 0
                for q in range(2):
                    n = 2 * i + (U0 + 1 + q)
                    zz_free(n)
                    gated(n, (1 + q) % 2)
                    xt_evac(n + 1 - U0, q % 2)
            own.base, own.n = 0, n2 + (NSLOT - 3)
            zz_free(NU - 2)
            gated(NU - 2, 1)
            xt_evac(NSLOT - 1, 0)
            zz_free(NU - 1)
            gated(NU - 1, 0)

            val = vg_sb[:, :, 0:G * HD].rearrange("p t (g d) -> p t g d", g=G)
            res = [vres[:, c].rearrange("p t (g d) -> p t g d", g=G) for c in range(2)]
            vp = [v_pack[:, :, :, c * HD:(c + 1) * HD] for c in range(3)]
            dve.wait_ge(const_ready, 1)
            for t in range(NT):
                own.did(V.tensor_copy(vp[0][:, t], val[:, t]))
            own.wait()
            for t in range(NT):
                own.did(V.tensor_tensor(res[0][:, t], val[:, t], vp[0][:, t], ALU.subtract))
            own.wait()
            for t in range(NT):
                own.did(V.tensor_copy(vp[1][:, t], res[0][:, t]))
            own.wait()
            for t in range(NT):
                own.did(V.tensor_tensor(res[1][:, t], res[0][:, t], vp[1][:, t], ALU.subtract))
            own.wait()
            for t in range(NT):
                V.tensor_copy(vp[2][:, t], res[1][:, t]).then_inc(v_ready, 1)

            V.memset(k_pack[32:64, :, :].bitcast(F32), 1.0).then_inc(own.sem, 1)
            V.memset(k_pack[96:128, :, :].bitcast(F32), 1.0).then_inc(own.sem, 1)
            own.n += 2
            own.wait()
            V.memset(negm[:, QT:2 * QT, :], 0.0).then_inc(ones_set, 1)

            def low_part(n, f):
                dve.wait_ge(hi_done, n + 1)
                V.tensor_tensor(stage[:, 1, f, :], bank(f % 2, T), stage[:, 0, f, :].bitcast(F32),
                                ALU.subtract).then_inc(lo_done, 1)

            for c in range(B):
                low_part(c, c)
            n3 = own.n
            with dve.Fori(0, B) as b:
                own.base, own.n = n3 + G * b, 0
                for f in range(QF):
                    low_part(QF * b + (B + f), f)
                for g in range(G):
                    for qt in range(QT):
                        dve.wait_ge(max_ps, QT * (G * b + g) + qt + 1)
                        banks = psum[:, 6:8, :] if qt == 0 else psum[:, 0:2, :]
                        s_ = banks.rearrange("p a (r n) -> p (a r) n", r=2)[:, :, 0:(qt + 1) * P]
                        V.tensor_reduce(negm[:, qt, REP * g:REP * g + REP], s_, AX.X, ALU.max,
                                        negate=True).then_inc(negm_done, 1)

                def context(g):
                    dve.wait_ge(pv_ps, G * b + g + 3)
                    sums = bank(5, QT * REP * VCOL).rearrange("p (c n) -> p c n", c=QT * REP)
                    own.did(V.reciprocal(den[:, :], sums[:, :, VCOL - 1]))
                    V.tensor_reduce(csum[:, :, :], sums[:, :, 0:3 * HD].rearrange("p c (j d) -> p c d j", j=3), AX.X,
                                    ALU.add).then_inc(csum_done, 1)
                    own.wait()
                    dve.wait_ge(csum_done, G * b + g + 2)
                    V.tensor_tensor(ctxs[:, :, g * REP * HD:(g + 1) * REP * HD].rearrange("p a (r d) -> p a r d", r=REP),
                                    csum[:, :, :].rearrange("p (a r) d -> p a r d", a=QT),
                                    den[:, :].rearrange("p (a r c) -> p a r c", a=QT, c=1).broadcast_to([P, QT, REP, HD]),
                                    ALU.mult).then_inc(ctx_done, 1)
                    dve.wait_ge(ctx_done, G * b + g + 1)

                for g in range(G):
                    dve.wait_ge(hi16_done, G * b + g + 1)
                    V.tensor_tensor(plo[:, g % 2, :], pexp[:, g % 2, :], phi[:, g % 2, :],
                                    ALU.subtract).then_inc(lo16_done, 1)
                    if g:
                        context(g - 1)
                context(G - 1)
                for qt in range(QT):
                    dve.wait_ge(wo_ps, QT * b + qt + 1)
                    dve.wait_ge(comb[TOPK - 1], 16 * (QT * b + qt + 1))
                    dve.wait_ge(out_dma[qt], 16 * b + 1)
                    V.tensor_tensor(osb[:, qt, :], acc[:, bass.ds(QT * b + qt, 1), :].rearrange("p a d -> p (a d)"),
                                    bank(qt), ALU.add).then_inc(out_sb, 1)

        @block.tensor
        def _(pe):
            MM, TR = nc.tensor.matmul, nc.tensor.transpose
            pe.sem_inc(st_ps, 1)
            pe.sem_inc(pv_ps, 2)
            pe.sem_inc(packed, 1)
            pe.wait_ge(const_ready, 1)
            for t in range(NT):
                pe.wait_ge(xn_ready, t + 1)
                if t >= 2:
                    pe.wait_ge(xnT_sb, t - 1)
                for k in range(KD):
                    last = TR(psum[:, t % 2, k * P:(k + 1) * P], xn[:, t, k * P:(k + 1) * P], ident[:, :])
                last.then_inc(xnT_ps, 1)
            pe.wait_ge(wvg_in, 16)
            for t in range(NT):
                pe.wait_ge(xnT_sb, t + 1)
                if t >= 2:
                    pe.wait_ge(vg_done, t - 1)
                for k in range(KD):
                    last = MM(bank(2 + t % 2, VG), xT[:, k, t * P:(t + 1) * P], wvg_sb[:, k, :], start=k == 0,
                              stop=k == KD - 1)
                last.then_inc(vg_ps, 1)

            def gate_up(n, par, lhs, weights):
                if not isinstance(n, int) or n >= 2:
                    pe.wait_ge(z_done, n - 1)
                for k in range(KD):
                    last = MM(bank(4 + par), lhs(k), weights(k * 2 * FI), start=k == 0, stop=k == KD - 1)
                last.then_inc(gu_ps, 1)

            def z_transpose(n, par):
                pe.wait_ge(z_done, n + 1)
                if not isinstance(n, int) or n >= 1:
                    pe.wait_ge(zt_sb, n)
                for k in range(FK):
                    last = TR(psum[:, 3, k * P:(k + 1) * P], zz[:, par, k * P:(k + 1) * P], ident[:, :])
                last.then_inc(zt_ps, 1)

            def down(n, par, weights):
                pe.wait_ge(zt_sb, n + 1)
                if not isinstance(n, int) or n >= U0:
                    pe.wait_ge(y_sb, n - U0 + 1)
                elif n >= 2:
                    pe.wait_ge(sh_sb, n - 1)
                for k in range(FK):
                    last = MM(bank(6 + par), zT[:, par, k, :], weights(GUC + k * D), start=k == 0, stop=k == FK - 1)
                last.then_inc(dn_ps, 1)

            def shared_w(c):
                return wbuf[:, NBUF - 1, c:c + 512]

            pe.wait_ge(we_in[NBUF - 1], 16)
            pe.wait_ge(vg_done, NT)
            pe.wait_ge(mask_ready, 1)
            all16 = mask16[:, :, :].rearrange("p t e -> p (t e)")
            MM(bank(0, NT * NE), before_b[:, :], all16, start=True, stop=False, skip_group_check=True)
            for i in range(NT - 1):
                last = MM(psum[:, 0, (i + 1) * NE:NT * NE].rearrange("p (t e) -> p t e", e=NE), ones_b[:, :],
                          mask16[:, i:i + 1, :].broadcast_to([P, NT - 1 - i, NE]), start=False,
                          stop=i == NT - 2, skip_group_check=True)
            last.then_inc(ranks_ps, 1)
            for i in range(NT):
                last = MM(bank(1, NE), ones_b[:, :], mask16[:, i, :], start=i == 0, stop=i == NT - 1)
            last.then_inc(ranks_ps, 1)
            for n in range(NT):
                if n:
                    z_transpose(n - 1, (n - 1) % 2)
                gate_up(n, n % 2, lambda k: xT[:, k, n * P:(n + 1) * P], shared_w)
                if n:
                    down(n - 1, (n - 1) % 2, shared_w)

            pe.wait_ge(slots_known, 1)

            def rows_transpose(s, par, count):
                pe.wait_ge(xg_in[par], count)
                if not isinstance(s, int) or s >= 1:
                    pe.wait_ge(xt_sb, s)
                for k in range(KD):
                    last = TR(psum[:, 2, k * P:(k + 1) * P], xg[:, par, k * P:(k + 1) * P], ident[:, :])
                last.then_inc(xt_ps, 1)

            def slot_weights(s):
                e = pe.value_load(sexp_i[0:1, 0, bass.ds(s, 1)], min_val=0, max_val=NE - 1)
                pl = pe.value_load(sexp_i[0:1, 4, bass.ds(s, 1)], min_val=0, max_val=NBUF - 1)
                pe.wait_ge(w_ready, e + 1)
                return lambda c: wbuf[:, bass.ds(pl, 1), c:c + 512].rearrange("p a n -> p (a n)")


            def slot_rows(par):
                return lambda k: xgT[:, par, k, :]

            rows_transpose(0, 0, 16)
            rows_transpose(1, 1, 16)
            z_transpose(U0 - 1, 1)
            weights = slot_weights(0)
            pe.wait_ge(xt_sb, 1)
            gate_up(U0, 0, slot_rows(0), weights)
            down(U0 - 1, 1, shared_w)
            pe.wait_ge(sh_sb, NT)
            def slot(s, par, more=None):
                n = s + U0
                if more is not None:
                    rows_transpose(s + 1, 1 - par, more)
                z_transpose(n - 1, 1 - par)
                now = slot_weights(s)
                pe.wait_ge(xt_sb, s + 1)
                gate_up(n, par, slot_rows(par), now)
                down(n - 1, 1 - par, slot_weights(s - 1))

            with pe.Fori(0, (NSLOT - 3) // 2) as i:
                slot(2 * i + 1, 1, 16 * i + 32)
                slot(2 * i + 2, 0, 16 * i + 32)
            slot(NSLOT - 2, 1, 16 * ((NSLOT + 1) // 2))
            slot(NSLOT - 1, 0)
            z_transpose(NU - 1, 0)
            down(NU - 1, 0, slot_weights(NSLOT - 1))

            pe.wait_ge(wqk_in, 16)
            pe.wait_ge(wo_in, 16)
            pe.wait_ge(v_ready, NT)
            pe.wait_ge(y_sb, NSLOT + 2)

            def project(n, f, first, col):
                pe.wait_ge(lo_done, n + 1)
                for k in range(KD):
                    last = MM(bank(f % 2, T), wqk_sb[:, k, col:col + P],
                              xT[:, k:k + 1, bass.ds(first, T)].rearrange("p a n -> p (a n)"), start=k == 0, stop=k == KD - 1)
                last.then_inc(qk_ps, 1)

            for c in range(B):
                project(c, c, c * T, QF * P)
            with pe.Fori(0, B) as b:
                pe.wait_ge(out_sb, QT * b + 1)
                for f in range(QF):
                    project(QF * b + (B + f), f, T * b, f * P)
                pe.wait_ge(packed, PACKS * (b + 1) + 1)
                for g in range(G):
                    lo = 64 * (g // 4)
                    for qt in range(QT):
                        pe.wait_ge(negm_done, QT * (G * b + g) + qt + 1)
                        for pr in range(2):
                            dst = 6 + pr if qt == 0 else pr
                            for r in range(2):
                                MM(psum[:, dst, r * T:(r + 1) * T],
                                   q_pack[lo:lo + QROWS, REP * (g % 4) + 2 * pr + r, qt * P:(qt + 1) * P],
                                   k_pack[lo:lo + QROWS, g % 4, :], start=r == 0, stop=False, skip_group_check=True)
                            last = MM(psum[:, dst, :].rearrange("p (r n) -> p r n", r=2)[:, :, qt * P:(qt + 1) * P],
                                      ident_b[:, :], mask_b[:, :].rearrange("p (a n) -> p a n", a=1).broadcast_to([P, 2, P]),
                                      start=False, stop=True, skip_group_check=True)
                        last.then_inc(max_ps, 1)
                pe.wait_ge(negm_done, QT * G * (b + 1) + 2)
                pe.wait_ge(csum_done, G * b + 1)
                TR(psum[:, 5, 0:P], negm[:, :, :].rearrange("p a h -> p (a h)"), ident[:, :]).then_inc(nmT_ps, 1)
                pe.wait_ge(nm_in, 64 * (b + 1))

                def weighted(g):
                    i = G * b + g
                    pe.wait_ge(lo16_done, i + 3)
                    pe.wait_ge(csum_done, i + 1)
                    for qt in range(QT):
                        for r in range(REP):
                            c = (qt * REP + r) * VCOL
                            parts = [(p_, kt) for kt in range(qt + 1) for p_ in (phi, plo)]
                            for m, (p_, kt) in enumerate(parts):
                                col = r * T + qt * P if kt == 0 else 2 * 512 + r * P
                                last = MM(psum[:, 5, c:c + VCOL], p_[:, g % 2, col:col + P],
                                          v_pack[:, QT * (g % B) + kt, bass.ds(2 * b + g // B, 1), 0:VCOL].rearrange("p a n -> p (a n)"),
                                          start=m == 0, stop=m == len(parts) - 1, skip_group_check=True)
                    last.then_inc(pv_ps, 1)

                for g in range(G):
                    lo, h0 = 64 * (g // 4), REP * (g % 4)
                    pe.wait_ge(exp_done, G * b + g + 1)
                    rows = slice(lo, lo + QROWS + 1)
                    for pr in range(2):
                        MM(psum[:, 2 + pr, :], k_pack[rows, g % 4, 0:P], q_pack[rows, h0 + 2 * pr:h0 + 2 * pr + 2, :],
                           start=True, stop=True)
                    MM(psum[:, 4, :], k_pack[rows, g % 4, P:T], q_pack[rows, h0:h0 + REP, P:T],
                       start=True, stop=True).then_inc(st_ps, 1)
                    if g:
                        weighted(g - 1)
                weighted(G - 1)
                pe.wait_ge(ctx_done, G * (b + 1))
                for qt in range(QT):
                    for k in range(KD):
                        last = TR(psum[:, 6 + qt, k * P:(k + 1) * P], ctxs[:, qt, k * P:(k + 1) * P], ident[:, :])
                    last.then_inc(ct_ps, 1)
                for qt in range(QT):
                    pe.wait_ge(ct_sb, QT * b + qt + 1)
                    for k in range(KD):
                        last = MM(bank(qt), ctxT[:, qt, k, :], wo_sb[:, k, :], start=k == 0, stop=k == KD - 1)
                    last.then_inc(wo_ps, 1)


def kernel(**inputs):
    import concourse.bacc as bacc
    import numpy as np
    from concourse.bass_utils import run_bass_kernel_spmd

    a = {name: np.asarray(v) for name, v in inputs.items()}

    def by_rows(w):
        return w.reshape(-1, P, w.shape[-1]).transpose(1, 0, 2)

    kv = a["L0_attn_Wkv"].reshape(D, G, 2, HD)
    wk, wv = kv[:, :, 0].reshape(D, G * HD), kv[:, :, 1].reshape(D, G * HD)
    gate = np.concatenate([a["L0_ffn_Wg"], a["L0_ffn_Sg"][None]])
    up = np.concatenate([a["L0_ffn_Wu"], a["L0_ffn_Su"][None]])
    down = np.concatenate([a["L0_ffn_Wd"], a["L0_ffn_Sd"][None]])
    gu = np.concatenate([gate.transpose(0, 2, 1), up.transpose(0, 2, 1)], axis=2)
    gu = gu.reshape(NE + 1, KD, P, 2 * FI).transpose(0, 2, 1, 3).reshape(NE + 1, P, GUC)
    dn = down.transpose(0, 2, 1).reshape(NE + 1, FK, P, D).transpose(0, 2, 1, 3).reshape(NE + 1, P, FK * D)
    laid = {
        "x": a["L0_attn_x"].reshape(NTOK, D),
        "wqk": by_rows(np.concatenate([a["L0_attn_Wq"], wk], axis=1)),
        "wvg": by_rows(np.concatenate([wv, a["L0_ffn_gate_w"].T], axis=1)),
        "wo": by_rows(a["L0_attn_Wo"]),
        "bo": a["L0_attn_bo"],
        "ebias": a["L0_ffn_bias"],
        "wexp": np.concatenate([gu, dn], axis=2),
    }
    laid = {name: np.ascontiguousarray(v) for name, v in laid.items()}
    nc = bacc.Bacc("TRN2", target_bir_lowering=False, num_devices=1)
    args = [nc.dram_tensor(name, v.shape, mybir.dt.from_np(v.dtype), kind="ExternalInput").ap() for name, v in laid.items()]
    out = nc.dram_tensor("out", (NTOK, D), F32, kind="ExternalOutput").ap()
    block_program(nc, *args, out)
    result = run_bass_kernel_spmd(nc, [laid], core_ids=[0])
    return result.results[0]["out"].reshape(B, T, D)
```

```python
from contextlib import ExitStack

import concourse.bass as bass
from concourse import mybir

F32 = mybir.dt.float32
F32R = mybir.dt.float32r
BF16 = mybir.dt.bfloat16
F16 = mybir.dt.float16
I32 = mybir.dt.int32
ALU = mybir.AluOpType
ACT = mybir.ActivationFunctionType
AX = mybir.AxisListType

P = 128
B, T, D = 4, 256, 512
NTOK = B * T
NT = NTOK // P
KD = D // P
H, G = 32, 8
HD = D // H
REP = H // G
QT = T // P
NE, TOPK, FI = 16, 4, 256
FK = FI // P
NSLOT = (TOPK * NTOK + (NE - TOPK) + NE * (P - 1)) // P
NBUF = 3
SPG = 2
NLOOP = B - 1
assert NLOOP * G * SPG >= NSLOT
NCOL = 1 + NLOOP * G * SPG + 2
WCOLS = KD * 2 * FI + FK * D
GUC = KD * 2 * FI
VG = G * HD + NE
QROWS = 3 * HD
VCOL = 3 * HD + 1
QF = H * HD // P
SCALE = HD ** -0.5
BIG = 1.0e30
EPS = 1e-5


class Steps:

    def __init__(self, eng, sem):
        self.eng, self.sem, self.base, self.n = eng, sem, 0, 0

    def did(self, instruction):
        instruction.then_inc(self.sem, 1)
        self.n += 1

    def wait(self):
        self.eng.wait_ge(self.sem, self.base + self.n)


def block_program(nc, x, wqk, wvg, wo, bo, ebias, wexp, out):
    table = nc.dram_tensor("slot_table", [P, NCOL * 2], F32, kind="Internal").ap()
    xn_rows = nc.dram_tensor("xn_rows", [NTOK, D], F32, kind="Internal").ap()
    q_parts = nc.dram_tensor("q_parts", [QF, P, 2, T], F32, kind="Internal").ap()
    k_parts = nc.dram_tensor("k_parts", [P, 2, NTOK], F32, kind="Internal").ap()
    y_rows = nc.dram_tensor("y_rows", [NLOOP * G * SPG * P, D], F32, kind="Internal").ap()

    ctx = ExitStack()
    with ctx:
        def sb(name, shape, dt):
            return ctx.enter_context(nc.sbuf_tensor(name, shape, dt))

        def sem(name):
            return ctx.enter_context(nc.semaphore(name))

        acc = sb("acc", [P, NT, D], F32)
        xn = sb("xn", [P, NT, D], F32)
        xT = sb("xT", [P, KD, NTOK], F32)
        wbuf = sb("wbuf", [P, NBUF, WCOLS], F32)
        wqk_sb = sb("wqk_sb", [P, KD, (H + G) * HD], F32)
        wvg_sb = sb("wvg_sb", [P, KD, VG], F32)
        wo_sb = sb("wo_sb", [P, KD, D], F32)
        bo_sb = sb("bo_sb", [P, D], F32)
        ebias_sb = sb("ebias_sb", [P, NE], F32)
        stage = sb("stage", [P, 2, QF, T], F32R)
        q_pack = sb("q_pack", [P, H // 2, T], F32R)
        k_pack = sb("k_pack", [P, B, T], F32R)
        v_pack = sb("v_pack", [P, NT, G, VCOL + 1], BF16)
        ident = sb("ident", [P, P], F32)
        ident_b = sb("ident_b", [P, P], BF16)
        mask_b = sb("mask_b", [P, P], BF16)
        before_b = sb("before_b", [P, P], BF16)
        ones_b = sb("ones_b", [P, P], BF16)
        ones_f = sb("ones_f", [P, NT * NE], F32)
        kcount = sb("kcount", [P, TOPK], F32)
        tile4 = sb("tile4", [P, NT], F32)
        lim = sb("lim", [P, NT - 1], F32)
        siota = sb("siota", [P, NCOL], F32)
        zeros = sb("zeros", [P, NCOL * 2], F32)
        gidx = sb("gidx", [P, 2], I32)
        gnone = sb("gnone", [P, 3], F32)
        xg = sb("xg", [P, 2, D], F32)
        xgT = sb("xgT", [P, 2, KD, P], F32)
        th = sb("th", [P, 2, FI], F32)
        zh = sb("zh", [P, FI], F32)
        zz = sb("zz", [P, 2, FI], F32)
        zT = sb("zT", [P, 2, FK, P], F32)
        ysb = sb("ysb", [P, 2, D], F32)
        xflat = xn[:, :, :].rearrange("p t d -> p (t d)")
        pexp = xflat[:, 0:3072].rearrange("p (b n) -> p b n", b=2)
        phi = sb("phi", [P, 2, 1536], F16)
        plo = sb("plo", [P, 2, 1536], F16)
        negm = sb("negm", [P, 2, QT, H // 2], F32)
        negmT = sb("negmT", [QT * H // 2, P], F32R)
        den = sb("den", [P, QT * REP], F32)
        csum = sb("csum", [P, QT * REP, HD], F32)
        ctxs = sb("ctxs", [P, QT, D], F32)
        ctxT = sb("ctxT", [P, QT, KD, P], F32)
        stats = sb("stats", [P, NT, 6], F32)
        mv = sb("mv", [P, NT, 2], F32)
        sm = sb("sm", [P, 7, NT], F32)
        vg_sb = sb("vg_sb", [P, NT, VG], F32)
        rt = xflat[:, 0:14 * NT * NE].rearrange("p (c t e) -> p c t e", c=14, t=NT)
        oh = xflat[:, 2048:4096].rearrange("p (c t k e) -> p c t k e", c=4, t=NT, k=TOPK)
        vres = xflat[:, 2048:4096].rearrange("p (c t n) -> p c t n", c=2, t=NT)
        top8 = sb("top8", [P, NT, 8], F32)
        need = sb("need", [P, 6, NT], F32)
        mask16 = sb("mask16", [P, NT, NE], BF16)
        ecount = sb("ecount", [P, 6, NE], F32)
        sgt = sb("sgt", [P, NE, NT - 1], F32)
        scmp = xflat[:, 3072:3072 + NCOL * NE].rearrange("p (s e) -> p s e", e=NE)
        sexp = sb("sexp", [P, 2, NCOL], F32)
        sexp_i = sb("sexp_i", [P, 5, NCOL], I32)
        where = sb("where", [P, NCOL, 2], I32)
        end_i = sb("end_i", [P, NE], I32)
        dest_f = sb("dest_f", [P, NT, TOPK], F32)
        dest_i = sb("dest_i", [P, NT, TOPK], I32)
        tpos_i = sb("tpos_i", [P, 4, NT, TOPK], I32)
        pair = sb("pair", [P, NT, TOPK, 2], F32)
        tab = sb("tab", [P, NCOL, 2], F32)

        psum = ctx.enter_context(nc.psum_tensor("psum", [P, 8, 512], F32))

        def bank(i, cols=512):
            return psum[:, i, 0:cols]

        def sems(names):
            return [sem(n) for n in names.split()]

        (const_ready, sqrt_in, sqrt_done, dve_step, pool_step, xn_ready, xnT_ps, xnT_sb, xn_stored, vg_ps, vg_done,
         rexp_done, mask_ready, ranks_ps, slots_known, pair_ready, table_zero, scattered, table_back, bo_added,
         v_ready) = sems(
            "const_ready sqrt_in sqrt_done dve_step pool_step xn_ready xnT_ps xnT_sb xn_stored vg_ps vg_done "
            "rexp_done mask_ready ranks_ps slots_known pair_ready table_zero scattered table_back bo_added v_ready")
        (xt_ps, xt_sb, gu_ps, th_done, z_done, zt_ps, zt_sb, dn_ps, y_sb, shared_done, w_ready) = sems(
            "xt_ps xt_sb gu_ps th_done z_done zt_ps zt_sb dn_ps y_sb shared_done w_ready")
        (proj_ps, hi_done, lo_done, ones_set, max_ps, negm_done, nmT_ps, nmT_sb, nm_in, st_ps, exp_done, masked,
         hi16_done, lo16_done, pv_ps, csum_done, ctx_done, ct_ps, ct_sb, wo_ps, att_added, k_out, stored) = sems(
            "proj_ps hi_done lo_done ones_set max_ps negm_done nmT_ps nmT_sb nm_in st_ps exp_done masked "
            "hi16_done lo16_done pv_ps csum_done ctx_done ct_ps ct_sb wo_ps att_added k_out stored")
        wvg_in, wqk_in, wo_in, small_in = sems("wvg_in wqk_in wo_in small_in")
        x_in = [sem(f"x_in{i}") for i in range(4)]
        we_in = [sem(f"we_in{i}") for i in range(NBUF)]
        xg_in = [sem(f"xg_in{i}") for i in range(2)]
        y_out = [sem(f"y_out{i}") for i in range(2)]
        parts_out = [sem(f"parts_out{i}") for i in range(QF)]
        packed = [sem(f"packed{i}") for i in range(2)]
        comb = [sem(f"comb{i}") for i in range(NT)]

        def arrivals(e):
            return e // NBUF + 1 + (e % NBUF == NBUF - 1)

        HALF_PACK = 9 * 16
        U1 = NT + 1
        GU, XT, DN, PV = 5, 6, 7, 4

        block = ctx.enter_context(nc.Block())

        def pack_half(eng, half, b):
            for row, (kpart, qpart) in enumerate(((0, 0), (1, 0), (0, 1))):
                base = 64 * half + HD * row
                eng.dma_start(k_pack[base:base + HD, :, :].rearrange("r c t -> r (c t)").bitcast(F32),
                              k_parts[bass.ds(2 * HD * b + half * HD, HD), kpart, :]).then_inc(packed[half], 16)
                for f in (2 * half, 2 * half + 1):
                    eng.dma_start(q_pack[base:base + HD, 8 * (f % 2):8 * (f % 2) + 8, :].bitcast(F32),
                                  q_parts[f, :, qpart, :].rearrange("(h r) t -> r h t", r=HD)).then_inc(packed[half], 16)

        @block.sync
        def _(sp):
            for i in range(4):
                sp.dma_start(acc[:, 2 * i:2 * i + 2, :],
                             x[2 * i * P:(2 * i + 2) * P, :].rearrange("(t p) d -> p t d", p=P)).then_inc(x_in[i], 16)
            sp.dma_start(wvg_sb[:, :, :], wvg).then_inc(wvg_in, 16)
            sp.dma_start(ebias_sb[:, :], ebias.rearrange("(a n) -> a n", a=1).broadcast_to([P, NE])).then_inc(small_in, 16)
            sp.dma_start(bo_sb[:, :], bo.rearrange("(a n) -> a n", a=1).broadcast_to([P, D])).then_inc(small_in, 16)
            sp.dma_start(wqk_sb[:, :, :], wqk).then_inc(wqk_in, 16)
            sp.dma_start(wbuf[:, NBUF - 1, :], wexp[NE]).then_inc(we_in[NBUF - 1], 16)
            for t in range(NT):
                sp.wait_ge(xn_ready, t + 1)
                sp.dma_start(xn_rows[t * P:(t + 1) * P, :], xn[:, t, :]).then_inc(xn_stored, 16)
            for c in range(B):
                sp.wait_ge(lo_done, c + 1)
                sp.dma_start(k_parts[:, :, c * T:(c + 1) * T], stage[:, :, c, :].bitcast(F32)).then_inc(k_out, 16)
            for f in range(QF):
                sp.wait_ge(lo_done, B + f + 1)
                sp.dma_start(q_parts[f], stage[:, :, f, :].bitcast(F32)).then_inc(parts_out[f], 16)
            for e in range(NBUF - 1):
                sp.dma_start(wbuf[:, e, :], wexp[e]).then_inc(we_in[e], 16)
            sp.wait_ge(k_out, 16 * B)
            sp.wait_ge(ones_set, 1)
            for half in range(2):
                for f in (2 * half, 2 * half + 1):
                    sp.wait_ge(parts_out[f], 16)
                pack_half(sp, half, 0)
            sp.dma_start(wo_sb[:, :, :], wo).then_inc(wo_in, 16)
            sp.wait_ge(scattered, 16 * NT * TOPK)
            sp.dma_start(tab[:, :, :].rearrange("p s c -> p (s c)"), table).then_inc(table_back, 16)
            sp.wait_ge(slots_known, 1)
            for e in range(NBUF - 1, NE):
                sp.wait_ge(we_in[(e - 2) % NBUF], 16 * arrivals(e - 2))
                sp.sem_inc(w_ready, 1)
                if e == NBUF - 1:
                    sp.wait_ge(dn_ps, NT)
                else:
                    last = sp.value_load(end_i[0:1, e - NBUF:e - NBUF + 1], min_val=1, max_val=NSLOT)
                    sp.wait_ge(dn_ps, last + U1)
                sp.dma_start(wbuf[:, e % NBUF, :], wexp[e]).then_inc(we_in[e % NBUF], 16)
            for e in (NE - 2, NE - 1):
                sp.wait_ge(we_in[e % NBUF], 16 * arrivals(e))
                sp.sem_inc(w_ready, 1)
            for j in range(NT):
                sp.wait_ge(comb[j], 16 * TOPK)
                sp.wait_ge(att_added, j + 2 if j >= NLOOP * QT else NLOOP * QT + 1)
                sp.dma_start(out[j * P:(j + 1) * P, :], acc[:, j, :]).then_inc(stored, 16)
            sp.wait_ge(stored, 16 * NT)

        @block.gpsimd
        def _(pool):
            own = Steps(pool, pool_step)
            pool.sem_inc(exp_done, 1)
            own.did(nc.gpsimd.memset(ident[:, :], 0.0))
            own.wait()
            own.did(nc.gpsimd.affine_select(out=ident[:, :], in_=ident[:, :], compare_op=ALU.not_equal, fill=1.0, base=0,
                                            pattern=[[-1, P]], channel_multiplier=1))
            own.wait()
            pool.sem_inc(const_ready, 1)
            own.did(nc.gpsimd.memset(ident_b[:, :], 0.0))
            own.did(nc.gpsimd.memset(mask_b[:, :], 0.0))
            own.did(nc.gpsimd.memset(before_b[:, :], 1.0))
            own.did(nc.gpsimd.memset(zeros[:, :], 0.0))
            own.did(nc.gpsimd.memset(ones_b[:, :], 1.0))
            own.did(nc.gpsimd.memset(ones_f[:, :], 1.0))
            own.wait()
            own.did(nc.gpsimd.affine_select(out=ident_b[:, :], in_=ident_b[:, :], compare_op=ALU.not_equal, fill=1.0,
                                            base=0, pattern=[[-1, P]], channel_multiplier=1))
            own.did(nc.gpsimd.affine_select(out=mask_b[:, :], in_=mask_b[:, :], compare_op=ALU.is_ge, fill=-BIG, base=0,
                                            pattern=[[-1, P]], channel_multiplier=1))
            own.did(nc.gpsimd.affine_select(out=before_b[:, :], in_=before_b[:, :], compare_op=ALU.is_gt, fill=0.0, base=0,
                                            pattern=[[1, P]], channel_multiplier=-1))
            for m, step, base in ((kcount, 1, 1), (tile4, TOPK, 0), (lim, P, P), (siota, 1, -1)):
                own.did(nc.gpsimd.iota(m[:, :], pattern=[[step, m.shape[1]]], base=base, channel_multiplier=0,
                                       allow_small_or_imprecise_dtypes=True))
            for k in range(TOPK):
                own.did(nc.gpsimd.iota(pair[:, :, k, 0].bitcast(I32), pattern=[[P, NT]], base=0, channel_multiplier=1))
            own.wait()
            pool.sem_inc(const_ready, 1)
            pool.dma_start(table, zeros[:, :]).then_inc(table_zero, 16)
            pool.wait_ge(xn_ready, NT)
            pool.wait_ge(small_in, 32)
            nc.gpsimd.tensor_tensor(acc[:, :, :], acc[:, :, :],
                                    bo_sb[:, :].rearrange("p (a d) -> p a d", a=1).broadcast_to([P, NT, D]),
                                    ALU.add).then_inc(bo_added, 1)
            pool.wait_ge(table_zero, 16)
            pool.wait_ge(pair_ready, 1)
            for j in range(NT):
                for k in range(TOPK):
                    nc.gpsimd.indirect_dma_start(
                        out=table.rearrange("p (s c) -> (p s) c", c=2),
                        out_offset=bass.IndirectOffsetOnAxis(ap=tpos_i[:, 3, j, k:k + 1], axis=0),
                        in_=pair[:, j, k, :], in_offset=None).then_inc(scattered, 16)
            pool.wait_ge(table_back, 16)
            pool.wait_ge(xn_stored, 16 * NT)

            def gather(s, par, free):
                if free is not None:
                    pool.wait_ge(xt_ps, free)
                own.did(nc.gpsimd.tensor_copy(gidx[:, par:par + 1], tab[:, bass.ds(s + 1, 1), 0].bitcast(I32)))
                own.wait()
                own.did(nc.gpsimd.tensor_tensor(gnone[:, par:par + 1], ones_f[:, 0:1], ones_f[:, 0:1], ALU.mult))
                nc.gpsimd.indirect_dma_start(
                    out=xg[:, par, :], out_offset=None, in_=xn_rows,
                    in_offset=bass.IndirectOffsetOnAxis(ap=gidx[:, par:par + 1], axis=0)).then_inc(xg_in[par], 16)

            def causal(b, g):
                pool.wait_ge(exp_done, G * b + g + 2)
                own.did(nc.gpsimd.tensor_tensor(gnone[:, 2:3], ones_f[:, 0:1], ones_f[:, 0:1], ALU.mult))
                first = pexp[:, g % 2, 0:1024].rearrange("p (r q) -> p r q", r=REP)[:, :, 0:P]
                second = pexp[:, g % 2, 1024:1536].rearrange("p (r q) -> p r q", r=REP)
                for block_ in (first, second):
                    nc.gpsimd.affine_select(out=block_, in_=block_, compare_op=ALU.is_ge, fill=0.0, base=0,
                                            pattern=[[0, REP], [1, P]], channel_multiplier=-1).then_inc(masked, 1)

            gather(0, 0, None)
            gather(1, 1, None)
            n0, each = own.n, G + 2 * SPG * G
            with pool.Fori(0, NLOOP) as b:
                own.base, own.n = n0 + each * b, 0
                for g in range(G):
                    causal(b, g)
                    for q in range(SPG):
                        s = SPG * G * b + (SPG * g + q)
                        gather(s + 2, q, s + 1)
                assert own.n == each
            for par in range(2):
                pool.wait_ge(y_out[par], 16 * NLOOP * G * SPG // 2 + 1)
            pool.wait_ge(att_added, NLOOP * QT + 1)
            own.base, own.n = 0, n0 + NLOOP * each
            sums = [(k, j) for k in range(TOPK) for j in range(NT)]
            for g in range(G):
                causal(NLOOP, g)
                for k, j in sums[TOPK * g:TOPK * g + TOPK]:
                    if k:
                        pool.wait_ge(comb[j], 16 * k)
                    nc.gpsimd.indirect_dma_start(
                        out=acc[:, j, :], out_offset=None, in_=y_rows,
                        in_offset=bass.IndirectOffsetOnAxis(ap=dest_i[:, j, k:k + 1], axis=0),
                        compute_op=ALU.add).then_inc(comb[j], 16)

        @block.scalar
        def _(act):
            S = nc.scalar.activation
            act.sem_inc(y_sb, 1)
            act.sem_inc(y_out[0], 1)
            act.sem_inc(y_out[1], 1)
            act.wait_ge(sqrt_in, 1)
            S(sm[:, 1, :], sm[:, 0, :], ACT.Sqrt).then_inc(sqrt_done, 1)
            for t in range(NT):
                act.wait_ge(xnT_ps, t + 1)
                S(xT[:, :, t * P:(t + 1) * P], bank(t % 2).rearrange("p (k n) -> p k n", k=KD),
                  ACT.Copy).then_inc(xnT_sb, 1)
            for t in range(NT):
                act.wait_ge(vg_ps, t + 1)
                S(vg_sb[:, t, :], bank(2 + t % 2, VG), ACT.Copy).then_inc(vg_done, 1)
            act.wait_ge(vg_done, NT)
            act.wait_ge(xn_stored, 16 * NT)
            S(rt[:, 0, :, :], vg_sb[:, :, G * HD:VG], ACT.Exp, scale=-1.0).then_inc(rexp_done, 1)

            def high_part(n, f, src):
                act.wait_ge(proj_ps, n + 1)
                S(stage[:, 0, f, :], src, ACT.Copy).then_inc(hi_done, 1)

            for n in range(B + QF):
                if n >= B:
                    act.wait_ge(k_out, 16 * B)
                high_part(n, n % QF, bank(n % 4, T))

            def tanh(n, par):
                act.wait_ge(gu_ps, n + 1 if isinstance(n, int) else n)
                if not isinstance(n, int) or n >= 2:
                    act.wait_ge(z_done, n - 1)
                S(th[:, par, :], bank(GU, FI), ACT.Tanh, scale=0.5).then_inc(th_done, 1)

            def zt_evac(n, par):
                act.wait_ge(zt_ps, n + 1)
                S(zT[:, par, :, :], bank(DN, FI).rearrange("p (k n) -> p k n", k=FK), ACT.Copy).then_inc(zt_sb, 1)

            def y_evac(s, par, count):
                act.wait_ge(dn_ps, s + (U1 + 1))
                act.wait_ge(y_out[par], count)
                S(ysb[:, par, :], bank(DN), ACT.Copy, scale=tab[:, bass.ds(s + 1, 1), 1]).then_inc(y_sb, 1)
                act.wait_ge(y_sb, s + 3)
                act.dma_start(y_rows[bass.ds((s + 1) * P, P), :], ysb[:, par, :]).then_inc(y_out[par], 16)

            for n in range(NT):
                if n:
                    zt_evac(n - 1, (n - 1) % 2)
                tanh(n, n % 2)
            zt_evac(NT - 1, 1)

            def minus_maxima(idx, half):
                act.wait_ge(nmT_ps, idx + 1)
                S(negmT[:, :], psum[0:QT * H // 2, 3, 0:P], ACT.Copy).then_inc(nmT_sb, 1)
                act.wait_ge(nmT_sb, idx + 1)
                for qt in range(QT):
                    act.dma_start(q_pack[64 * half + QROWS:64 * half + QROWS + 1, :, qt * P:(qt + 1) * P].bitcast(F32),
                                  negmT[qt * H // 2:(qt + 1) * H // 2, :].bitcast(F32)).then_inc(nm_in, 16)

            minus_maxima(0, 0)
            act.wait_ge(table_back, 16)

            def numerators(b, g):
                act.wait_ge(st_ps, G * b + g + 1)
                act.wait_ge(lo16_done, G * b + g + 1)
                S(pexp[:, g % 2, :], psum[:, 0:3, :].rearrange("p a n -> p (a n)"), ACT.Exp,
                  scale=SCALE).then_inc(exp_done, 1)

            def high16(b, g):
                act.wait_ge(masked, 2 * (G * b + g + 1))
                act.wait_ge(pv_ps, G * b + g + 1)
                S(phi[:, g % 2, :], pexp[:, g % 2, :], ACT.Copy).then_inc(hi16_done, 1)

            def context_evac(b):
                for qt in range(QT):
                    act.wait_ge(ct_ps, QT * b + qt + 1)
                    S(ctxT[:, qt, :, :], bank(qt).rearrange("p (k n) -> p k n", k=KD), ACT.Copy).then_inc(ct_sb, 1)

            with act.Fori(0, NLOOP) as b:
                for g in range(G):
                    s = SPG * G * b + SPG * g
                    if g == 4:
                        for f in (0, 1):
                            act.wait_ge(parts_out[f], 16 * b + 32)
                        pack_half(act, 0, b + 1)
                    numerators(b, g)
                    if g < QF:
                        high_part(QF * b + (B + QF + g), g, bank(3, T))
                    zt_evac(s + (U1 - 1), 1)
                    high16(b, g)
                    tanh(s + U1, 0)
                    if g < QF:
                        act.wait_ge(lo_done, QF * b + (B + QF + g + 1))
                        act.dma_start(q_parts[g], stage[:, :, g, :].bitcast(F32)).then_inc(parts_out[g], 16)
                    y_evac(s - 1, 1, 16 * (G * b + g) + 1)
                    zt_evac(s + U1, 0)
                    if g in (3, 7):
                        minus_maxima(2 * b + (g // 4 + 1), 1 - g // 4)
                    tanh(s + (U1 + 1), 1)
                    y_evac(s, 0, 16 * (G * b + g) + 1)
                context_evac(b)
                for f in (2, 3):
                    act.wait_ge(parts_out[f], 16 * b + 32)
                pack_half(act, 1, b + 1)
            b = NLOOP
            for g in range(G):
                numerators(b, g)
                high16(b, g)
                if g == 3:
                    minus_maxima(2 * b + 1, 1)
            context_evac(b)

        @block.vector
        def _(dve):
            own = Steps(dve, dve_step)
            V = nc.vector

            def op(ins):
                own.did(ins)
                own.wait()

            dve.sem_inc(lo16_done, 2)
            dve.sem_inc(csum_done, 1)
            dve.sem_inc(att_added, 1)
            own.did(V.memset(k_pack[32:64, :, :].bitcast(F32), 1.0))
            own.did(V.memset(k_pack[96:128, :, :].bitcast(F32), 1.0))
            own.did(V.memset(v_pack[:, :, :, 3 * HD:VCOL + 1], 1.0))
            for t in range(NT):
                dve.wait_ge(x_in[t // 2], 16)
                own.did(V.bn_stats(stats[:, t, :], acc[:, t, :]))
            own.wait()
            for t in range(NT):
                own.did(V.bn_aggr(mv[:, t, :], stats[:, t, :]))
            own.wait()
            V.tensor_scalar(sm[:, 0, :], mv[:, :, 1], EPS, None, ALU.add).then_inc(sqrt_in, 1)
            dve.wait_ge(sqrt_done, 1)
            op(V.reciprocal(sm[:, 2, :], sm[:, 1, :]))
            op(V.tensor_tensor(sm[:, 3, :], sm[:, 2, :], sm[:, 2, :], ALU.mult))
            op(V.tensor_tensor(sm[:, 4, :], sm[:, 3, :], sm[:, 0, :], ALU.mult))
            op(V.tensor_scalar(sm[:, 5, :], sm[:, 4, :], -0.5, 1.5, ALU.mult, ALU.add))
            op(V.tensor_tensor(sm[:, 6, :], sm[:, 5, :], sm[:, 2, :], ALU.mult))
            for t in range(NT):
                V.tensor_scalar(xn[:, t, :], acc[:, t, :], mv[:, t, 0:1], sm[:, 6, t:t + 1], ALU.subtract,
                                ALU.mult).then_inc(xn_ready, 1)

            def over_experts(a):
                return a.rearrange("p (t a) -> p t a", a=1).broadcast_to([P, NT, NE])

            dve.wait_ge(const_ready, 2)
            dve.wait_ge(rexp_done, 1)
            dve.wait_ge(small_in, 32)
            op(V.tensor_scalar(rt[:, 1, :, :], rt[:, 0, :, :], 1.0, None, ALU.add))
            op(V.reciprocal(rt[:, 2, :, :], rt[:, 1, :, :]))
            score = rt[:, 3, :, :]
            op(V.tensor_tensor(score, rt[:, 2, :, :],
                               ebias_sb[:, :].rearrange("p (a e) -> p a e", a=1).broadcast_to([P, NT, NE]), ALU.add))
            for t in range(NT):
                own.did(V.max(top8[:, t, :], score[:, t, :]))
            own.wait()
            fourth = top8[:, :, TOPK - 1:TOPK].broadcast_to([P, NT, NE])
            above, equal = rt[:, 4, :, :], rt[:, 5, :, :]
            own.did(V.tensor_tensor(above, score, fourth, ALU.is_gt))
            op(V.tensor_tensor(equal, score, fourth, ALU.is_equal))
            own.did(V.tensor_reduce(need[:, 0, :], above, AX.X, ALU.add))
            flat = lambda a: a.rearrange("p t e -> p (t e)")
            op(V.tensor_tensor_scan(flat(rt[:, 6, :, :]), ones_f[:, :], flat(equal), 0.0, ALU.mult, ALU.add))
            own.did(V.tensor_scalar(need[:, 1, :], need[:, 0, :], -1.0, float(TOPK), ALU.mult, ALU.add))
            op(V.tensor_tensor(need[:, 2, :], rt[:, 6, :, 0], equal[:, :, 0], ALU.subtract))
            op(V.tensor_tensor(need[:, 3, :], need[:, 1, :], need[:, 2, :], ALU.add))
            op(V.tensor_tensor(rt[:, 7, :, :], rt[:, 6, :, :], over_experts(need[:, 3, :]), ALU.is_le))
            op(V.tensor_tensor(rt[:, 8, :, :], rt[:, 7, :, :], equal, ALU.mult))
            chosen = rt[:, 9, :, :]
            op(V.tensor_tensor(chosen, rt[:, 8, :, :], above, ALU.add))
            V.tensor_copy(mask16[:, :, :], chosen).then_inc(mask_ready, 1)
            own.did(V.tensor_tensor_scan(flat(rt[:, 10, :, :]), ones_f[:, :], flat(chosen), 0.0, ALU.mult, ALU.add))
            op(V.tensor_tensor(rt[:, 11, :, :], chosen, score, ALU.mult))
            own.did(V.tensor_tensor(rt[:, 12, :, :], rt[:, 10, :, :], over_experts(tile4[:, :]), ALU.subtract))
            op(V.tensor_reduce(need[:, 4, :], rt[:, 11, :, :], AX.X, ALU.add))
            op(V.tensor_scalar(need[:, 4, :], need[:, 4, :], 1e-20, None, ALU.add))
            op(V.reciprocal(need[:, 5, :], need[:, 4, :]))
            op(V.tensor_tensor(rt[:, 13, :, :], rt[:, 11, :, :], over_experts(need[:, 5, :]), ALU.mult))

            def per_choice(a):
                return a.rearrange("p t (a e) -> p t a e", a=1).broadcast_to([P, NT, TOPK, NE])

            op(V.tensor_tensor(oh[:, 0], per_choice(rt[:, 12, :, :]),
                               kcount[:, :].rearrange("p (a k c) -> p a k c", a=1, c=1).broadcast_to([P, NT, TOPK, NE]),
                               ALU.is_equal))
            op(V.tensor_tensor(oh[:, 1], oh[:, 0], per_choice(chosen), ALU.mult))
            op(V.tensor_tensor(oh[:, 2], oh[:, 1], per_choice(rt[:, 13, :, :]), ALU.mult))
            op(V.tensor_reduce(pair[:, :, :, 1], oh[:, 2], AX.X, ALU.add))
            def low_part(n, f, src):
                dve.wait_ge(hi_done, n + 1)
                V.tensor_tensor(stage[:, 1, f, :], src, stage[:, 0, f, :].bitcast(F32), ALU.subtract).then_inc(lo_done, 1)

            for n in range(B + QF):
                low_part(n, n % QF, bank(n % 4, T))
            dve.wait_ge(lo_done, 1)
            V.memset(negm[:, :, :, :], 0.0).then_inc(ones_set, 1)

            dve.wait_ge(ranks_ps, 2)
            op(V.tensor_copy(ecount[:, 0, :], bank(XT, NE)))
            by_limit = [P, NE, NT - 1]
            op(V.tensor_tensor(sgt[:, :, :], ecount[:, 0, :].rearrange("p (e a) -> p e a", a=1).broadcast_to(by_limit),
                               lim[:, :].rearrange("p (a m) -> p a m", a=1).broadcast_to(by_limit), ALU.is_gt))
            op(V.tensor_reduce(ecount[:, 1, :], sgt[:, :, :], AX.X, ALU.add))
            op(V.tensor_scalar(ecount[:, 2, :], ecount[:, 1, :], 1.0, None, ALU.add))
            op(V.tensor_tensor_scan(ecount[:, 3, :], ones_f[:, 0:NE], ecount[:, 2, :], 0.0, ALU.mult, ALU.add))
            op(V.tensor_tensor(ecount[:, 4, :], ecount[:, 3, :], ecount[:, 2, :], ALU.subtract))
            op(V.tensor_scalar(ecount[:, 5, :], ecount[:, 4, :], 1.0, float(P), ALU.add, ALU.mult))
            op(V.tensor_tensor(rt[:, 1, :, :], bank(PV, NT * NE).rearrange("p (t e) -> p t e", t=NT),
                               ecount[:, 5, :].rearrange("p (a e) -> p a e", a=1).broadcast_to([P, NT, NE]), ALU.add))
            op(V.tensor_tensor(oh[:, 3], oh[:, 1], per_choice(rt[:, 1, :, :]), ALU.mult))
            op(V.tensor_reduce(dest_f[:, :, :], oh[:, 3], AX.X, ALU.add))
            op(V.tensor_copy(dest_i[:, :, :], dest_f[:, :, :]))
            own.did(V.tensor_scalar(tpos_i[:, 0], dest_i[:, :, :], 7, None, ALU.arith_shift_right))
            op(V.tensor_scalar(tpos_i[:, 1], dest_i[:, :, :], P - 1, None, ALU.bitwise_and))
            op(V.tensor_scalar(tpos_i[:, 2], tpos_i[:, 1], float(NCOL), None, ALU.mult))
            V.tensor_tensor(tpos_i[:, 3], tpos_i[:, 2], tpos_i[:, 0], ALU.add).then_inc(pair_ready, 1)
            by_slot = [P, NCOL, NE]
            op(V.tensor_tensor(scmp[:, :, :], siota[:, :].rearrange("p (s a) -> p s a", a=1).broadcast_to(by_slot),
                               ecount[:, 3, :].rearrange("p (a e) -> p a e", a=1).broadcast_to(by_slot), ALU.is_ge))
            op(V.tensor_reduce(sexp[:, 0, :], scmp[:, :, :], AX.X, ALU.add))
            op(V.tensor_scalar(sexp[:, 1, :], sexp[:, 0, :], float(NE - 1), None, ALU.min))
            op(V.tensor_copy(sexp_i[:, 0, :], sexp[:, 1, :]))
            op(V.tensor_scalar(sexp_i[:, 1, :], sexp_i[:, 0, :], 11.0, None, ALU.mult))
            op(V.tensor_scalar(sexp_i[:, 2, :], sexp_i[:, 1, :], 5, None, ALU.arith_shift_right))
            op(V.tensor_scalar(sexp_i[:, 3, :], sexp_i[:, 2, :], -float(NBUF), None, ALU.mult))
            own.did(V.tensor_tensor(where[:, :, 0], sexp_i[:, 3, :], sexp_i[:, 0, :], ALU.add))
            own.did(V.tensor_scalar(where[:, :, 1], sexp_i[:, 0, :], 1.0, None, ALU.add))
            op(V.tensor_copy(end_i[:, :], ecount[:, 3, :]))
            V.tensor_copy(sexp_i[:, 4, :], sexp_i[:, 0, :]).then_inc(slots_known, 1)

            val = vg_sb[:, :, 0:G * HD].rearrange("p t (g d) -> p t g d", g=G)
            res = [vres[:, c].rearrange("p t (g d) -> p t g d", g=G) for c in range(2)]
            vp = [v_pack[:, :, :, c * HD:(c + 1) * HD] for c in range(3)]

            def split_value(c):
                if c < 2:
                    op(V.tensor_copy(vp[c], val if c == 0 else res[c - 1]))
                    op(V.tensor_tensor(res[c], val if c == 0 else res[c - 1], vp[c], ALU.subtract))
                else:
                    V.tensor_copy(vp[c], res[c - 1]).then_inc(v_ready, 1)

            def gated(n, par):
                dve.wait_ge(th_done, n + 1 if isinstance(n, int) else n)
                if not isinstance(n, int) or n:
                    dve.wait_ge(z_done, n)
                own.did(V.scalar_tensor_tensor(out=zh[:, :], in0=th[:, par, :], scalar=1.0, in1=bank(GU, FI),
                                               op0=ALU.add, op1=ALU.mult))
                own.wait()
                if not isinstance(n, int) or n >= 2:
                    dve.wait_ge(zt_ps, n - 1)
                V.scalar_tensor_tensor(out=zz[:, par, :], in0=zh[:, :], scalar=0.5, in1=psum[:, GU, FI:2 * FI],
                                       op0=ALU.mult, op1=ALU.mult).then_inc(z_done, 1)

            def shared_out(n):
                dve.wait_ge(dn_ps, n + 1)
                dve.wait_ge(bo_added, 1)
                V.tensor_tensor(acc[:, n, :], acc[:, n, :], bank(DN), ALU.add).then_inc(shared_done, 1)

            for n in range(NT):
                gated(n, n % 2)
                if n:
                    shared_out(n - 1)
                if n in (1, 3, 5):
                    split_value(n // 2)
            shared_out(NT - 1)
            dve.wait_ge(zt_ps, NT)
            dve.wait_ge(z_done, NT)
            V.memset(zz[:, 1, :], 0.0).then_inc(z_done, 1)

            def xt_evac(s, par):
                dve.wait_ge(xt_ps, s + 1)
                V.tensor_copy(xgT[:, par, :, :], bank(XT).rearrange("p (k n) -> p k n", k=KD)).then_inc(xt_sb, 1)

            def maxima(m, g):
                for qt in range(QT):
                    dve.wait_ge(max_ps, QT * m + qt + 1)
                    s_ = psum[:, 2 * qt:2 * qt + 2, :].rearrange("p a (r n) -> p (a r) n", r=2)[:, :, 0:(qt + 1) * P]
                    V.tensor_reduce(negm[:, g // 4, qt, REP * (g % 4):REP * (g % 4) + REP], s_, AX.X, ALU.max,
                                    negate=True).then_inc(negm_done, 1)

            def low16(b, g):
                dve.wait_ge(hi16_done, G * b + g + 1)
                V.tensor_tensor(plo[:, g % 2, :], pexp[:, g % 2, :], phi[:, g % 2, :], ALU.subtract).then_inc(lo16_done, 1)

            def context(b, g):
                i = G * b + g
                dve.wait_ge(pv_ps, i + 3)
                sums = bank(PV, QT * REP * VCOL).rearrange("p (c n) -> p c n", c=QT * REP)
                own.did(V.reciprocal(den[:, :], sums[:, :, VCOL - 1]))
                V.tensor_reduce(csum[:, :, :], sums[:, :, 0:3 * HD].rearrange("p c (j d) -> p c d j", j=3), AX.X,
                                ALU.add).then_inc(csum_done, 1)
                own.wait()
                dve.wait_ge(csum_done, i + 2)
                V.tensor_tensor(ctxs[:, :, g * REP * HD:(g + 1) * REP * HD].rearrange("p a (r d) -> p a r d", r=REP),
                                csum[:, :, :].rearrange("p (a r) d -> p a r d", a=QT),
                                den[:, :].rearrange("p (a r c) -> p a r c", a=QT, c=1).broadcast_to([P, QT, REP, HD]),
                                ALU.mult).then_inc(ctx_done, 1)
                dve.wait_ge(ctx_done, i + 1)

            def attention_out(b):
                for qt in range(QT):
                    dve.wait_ge(wo_ps, QT * b + qt + 1)
                    if isinstance(b, int):
                        dve.wait_ge(comb[QT * b + qt], 16 * TOPK)
                    tile = acc[:, bass.ds(QT * b + qt, 1), :].rearrange("p a d -> p (a d)")
                    V.tensor_tensor(tile, tile, bank(2 + qt), ALU.add).then_inc(att_added, 1)

            for g in range(4):
                maxima(g, g)
            xt_evac(0, 0)
            n3, each = own.n, G + SPG * G
            with dve.Fori(0, NLOOP) as b:
                own.base, own.n = n3 + each * b, 0
                for g in range(G):
                    s = SPG * G * b + SPG * g
                    if g < QF:
                        low_part(QF * b + (B + QF + g), g, bank(3, T))
                    xt_evac(s + 1, 1)
                    low16(b, g)
                    gated(s + U1, 0)
                    maxima(G * b + (g + 4), (g + 4) % G)
                    if g:
                        context(b, g - 1)
                    if g == G - 1:
                        context(b, g)
                    xt_evac(s + 2, 0)
                    gated(s + (U1 + 1), 1)
                attention_out(b)
                assert own.n == each
            own.base, own.n = 0, n3 + NLOOP * each
            b = NLOOP
            for g in range(G):
                low16(b, g)
                if g < 4:
                    maxima(G * b + (g + 4), (g + 4) % G)
                if g:
                    context(b, g - 1)
            context(b, G - 1)
            attention_out(b)

        @block.tensor
        def _(pe):
            MM, TR = nc.tensor.matmul, nc.tensor.transpose
            pe.sem_inc(pv_ps, 2)
            pe.wait_ge(const_ready, 1)
            for t in range(NT):
                pe.wait_ge(xn_ready, t + 1)
                if t >= 2:
                    pe.wait_ge(xnT_sb, t - 1)
                for k in range(KD):
                    last = TR(psum[:, t % 2, k * P:(k + 1) * P], xn[:, t, k * P:(k + 1) * P], ident[:, :])
                last.then_inc(xnT_ps, 1)
            pe.wait_ge(wvg_in, 16)
            for t in range(NT):
                pe.wait_ge(xnT_sb, t + 1)
                if t >= 2:
                    pe.wait_ge(vg_done, t - 1)
                for k in range(KD):
                    last = MM(bank(2 + t % 2, VG), xT[:, k, t * P:(t + 1) * P], wvg_sb[:, k, :], start=k == 0,
                              stop=k == KD - 1)
                last.then_inc(vg_ps, 1)

            def project(dst, first, col):
                for k in range(KD):
                    last = MM(dst, wqk_sb[:, k, col:col + P],
                              xT[:, k:k + 1, bass.ds(first, T)].rearrange("p a n -> p (a n)"), start=k == 0, stop=k == KD - 1)
                last.then_inc(proj_ps, 1)

            pe.wait_ge(wqk_in, 16)
            pe.wait_ge(vg_done, NT)
            for n in range(B + QF):
                if n >= 4:
                    pe.wait_ge(lo_done, n - 3)
                if n < B:
                    project(bank(n % 4, T), n * T, QF * P)
                else:
                    project(bank(n % 4, T), 0, (n - B) * P)

            pe.wait_ge(const_ready, 2)
            pe.wait_ge(mask_ready, 1)
            MM(bank(PV, NT * NE), before_b[:, :], mask16[:, :, :].rearrange("p t e -> p (t e)"), start=True, stop=False,
               skip_group_check=True)
            for i in range(NT - 1):
                last = MM(psum[:, PV, (i + 1) * NE:NT * NE].rearrange("p (t e) -> p t e", e=NE), ones_b[:, :],
                          mask16[:, i:i + 1, :].broadcast_to([P, NT - 1 - i, NE]), start=False,
                          stop=i == NT - 2, skip_group_check=True)
            last.then_inc(ranks_ps, 1)
            for i in range(NT):
                last = MM(bank(XT, NE), ones_b[:, :], mask16[:, i, :], start=i == 0, stop=i == NT - 1)
            last.then_inc(ranks_ps, 1)

            def gate_up(lhs, weights):
                for k in range(KD):
                    last = MM(bank(GU), lhs(k), weights(k * 2 * FI), start=k == 0, stop=k == KD - 1)
                last.then_inc(gu_ps, 1)

            def z_transpose(n, par):
                pe.wait_ge(z_done, n + 1)
                for k in range(FK):
                    last = TR(psum[:, DN, k * P:(k + 1) * P], zz[:, par, k * P:(k + 1) * P], ident[:, :])
                last.then_inc(zt_ps, 1)

            def down(n, par, weights):
                pe.wait_ge(zt_sb, n + 1)
                for k in range(FK):
                    last = MM(bank(DN), zT[:, par, k, :], weights(GUC + k * D), start=k == 0, stop=k == FK - 1)
                last.then_inc(dn_ps, 1)

            def shared_w(c):
                return wbuf[:, NBUF - 1, c:c + 512]

            pe.wait_ge(we_in[NBUF - 1], 16)
            for n in range(NT):
                if n:
                    if n >= 2:
                        pe.wait_ge(shared_done, n - 1)
                    z_transpose(n - 1, (n - 1) % 2)
                gate_up(lambda k: xT[:, k, n * P:(n + 1) * P], shared_w)
                if n:
                    down(n - 1, (n - 1) % 2, shared_w)
            pe.wait_ge(shared_done, NT - 1)
            z_transpose(NT - 1, 1)
            down(NT - 1, 1, shared_w)

            def scores_for_max(b, m, g, lo_count=None):
                lo = 64 * (g // 4)
                if lo_count is not None:
                    pe.wait_ge(lo_done, lo_count)
                for qt in range(QT):
                    for pr in range(2):
                        dst = 2 * qt + pr
                        for r in range(2):
                            MM(psum[:, dst, r * T:(r + 1) * T],
                               q_pack[lo:lo + QROWS, REP * (g % 4) + 2 * pr + r, qt * P:(qt + 1) * P],
                               k_pack[lo:lo + QROWS, g % 4, :], start=r == 0, stop=False, skip_group_check=True)
                        last = MM(psum[:, dst, :].rearrange("p (r n) -> p r n", r=2)[:, :, qt * P:(qt + 1) * P],
                                  ident_b[:, :], mask_b[:, :].rearrange("p (a n) -> p a n", a=1).broadcast_to([P, 2, P]),
                                  start=False, stop=True, skip_group_check=True)
                    last.then_inc(max_ps, 1)

            def maxima_transpose(steps, half):
                pe.wait_ge(negm_done, 2 * steps)
                TR(psum[0:QT * H // 2, 3, 0:P], negm[:, half, :, :].rearrange("p a h -> p (a h)"),
                   ident[:, :]).then_inc(nmT_ps, 1)

            def scores(b, g, max_steps):
                lo, h0 = 64 * (g // 4), REP * (g % 4)
                pe.wait_ge(exp_done, G * b + g + 1)
                pe.wait_ge(negm_done, 2 * max_steps)
                if g % 4 == 0:
                    pe.wait_ge(nm_in, 32 * (2 * b + g // 4 + 1))
                if g == 0:
                    pe.wait_ge(att_added, QT * b + 1)
                rows = slice(lo, lo + QROWS + 1)
                for pr in range(2):
                    MM(psum[:, pr, :], k_pack[rows, g % 4, 0:P], q_pack[rows, h0 + 2 * pr:h0 + 2 * pr + 2, :],
                       start=True, stop=True)
                MM(psum[:, 2, :], k_pack[rows, g % 4, P:T], q_pack[rows, h0:h0 + REP, P:T],
                   start=True, stop=True).then_inc(st_ps, 1)

            def weighted(b, g):
                i = G * b + g
                pe.wait_ge(lo16_done, i + 3)
                pe.wait_ge(csum_done, i + 1)
                for qt in range(QT):
                    for r in range(REP):
                        c = (qt * REP + r) * VCOL
                        parts = [(p_, kt) for kt in range(qt + 1) for p_ in (phi, plo)]
                        for m, (p_, kt) in enumerate(parts):
                            col = r * T + qt * P if kt == 0 else 2 * 512 + r * P
                            last = MM(psum[:, PV, c:c + VCOL], p_[:, g % 2, col:col + P],
                                      v_pack[:, QT * (g % B) + kt, bass.ds(2 * b + g // B, 1), 0:VCOL]
                                      .rearrange("p a n -> p (a n)"),
                                      start=m == 0, stop=m == len(parts) - 1, skip_group_check=True)
                last.then_inc(pv_ps, 1)

            def output_projection(b, nm_count):
                pe.wait_ge(ctx_done, G * (b + 1))
                pe.wait_ge(exp_done, G * (b + 1) + 1)
                for qt in range(QT):
                    for k in range(KD):
                        last = TR(psum[:, qt, k * P:(k + 1) * P], ctxs[:, qt, k * P:(k + 1) * P], ident[:, :])
                    last.then_inc(ct_ps, 1)
                pe.wait_ge(nmT_sb, nm_count)
                for qt in range(QT):
                    pe.wait_ge(ct_sb, QT * b + qt + 1)
                    for k in range(KD):
                        last = MM(bank(2 + qt), ctxT[:, qt, k, :], wo_sb[:, k, :], start=k == 0, stop=k == KD - 1)
                    last.then_inc(wo_ps, 1)

            pe.wait_ge(lo_done, B + QF)
            pe.wait_ge(packed[0], HALF_PACK)
            for g in range(4):
                if g:
                    pe.wait_ge(negm_done, 2 * g)
                scores_for_max(0, g, g)
            maxima_transpose(4, 0)

            def rows_transpose(s, par, count):
                pe.wait_ge(xg_in[par], count)
                if not isinstance(s, int) or s:
                    pe.wait_ge(xt_sb, s)
                for k in range(KD):
                    last = TR(psum[:, XT, k * P:(k + 1) * P], xg[:, par, k * P:(k + 1) * P], ident[:, :])
                last.then_inc(xt_ps, 1)

            def weights_at(place):
                return lambda c: wbuf[:, bass.ds(place, 1), c:c + 512].rearrange("p a n -> p (a n)")

            pe.wait_ge(slots_known, 1)
            rows_transpose(0, 0, 16)
            pe.wait_ge(wo_in, 16)
            pe.wait_ge(v_ready, 1)
            pe.wait_ge(shared_done, NT)
            with pe.Fori(0, NLOOP) as b:
                s0 = SPG * G * b
                prev = pe.value_load(where[0:1, bass.ds(s0, 1), 0], min_val=0, max_val=NBUF - 1)
                for g in range(G):
                    scores(b, g, G * b + (g + 4))
                    if g < QF:
                        project(bank(3, T), T * (b + 1), g * P)
                    for q in range(SPG):
                        s = s0 + (SPG * g + q)
                        place = pe.value_load(where[0:1, bass.ds(s + 1, 1), 0], min_val=0, max_val=NBUF - 1)
                        number = pe.value_load(where[0:1, bass.ds(s + 1, 1), 1], min_val=1, max_val=NE)
                        rows_transpose(s + 1, 1 - q, 16 * (G * b + g) + (16 + 16 * q))
                        pe.wait_ge(y_sb, s + 1)
                        z_transpose(s + (U1 - 1), 1 - q)
                        if q and g in (3, 7):
                            maxima_transpose(G * b + (g + 5), 1 - g // 4)
                        pe.wait_ge(w_ready, number)
                        pe.wait_ge(xt_sb, s + 1)
                        gate_up(lambda k: xgT[:, q, k, :], weights_at(place))
                        if q == 0:
                            pe.wait_ge(exp_done, G * b + g + 2)
                            half = 1 - g // 4
                            if g % 4 == 0:
                                pe.wait_ge(packed[half], HALF_PACK * (b + 2 - half))
                            scores_for_max(b, G * b + (g + 4), (g + 4) % G,
                                           QF * b + (B + QF + g + 1) if g < QF else None)
                        down(s + (U1 - 1), 1 - q, weights_at(prev))
                        if q == 0:
                            if g:
                                weighted(b, g - 1)
                            if g == G - 1:
                                weighted(b, g)
                        prev = place
                output_projection(b, 2 * b + 3)
            b = NLOOP
            for g in range(G):
                scores(b, g, G * b + min(g + 4, G))
                if g < 4:
                    pe.wait_ge(exp_done, G * b + g + 2)
                    if g == 0:
                        pe.wait_ge(packed[1], HALF_PACK * (b + 1))
                    scores_for_max(b, G * b + (g + 4), (g + 4) % G)
                if g == 3:
                    maxima_transpose(G * b + 8, 1)
                if g:
                    weighted(b, g - 1)
            weighted(b, G - 1)
            output_projection(b, 2 * b + 2)


def kernel(**inputs):
    import concourse.bacc as bacc
    import numpy as np
    from concourse.bass_utils import run_bass_kernel_spmd

    a = {name: np.asarray(v) for name, v in inputs.items()}

    def by_rows(w):
        return w.reshape(-1, P, w.shape[-1]).transpose(1, 0, 2)

    kv = a["L0_attn_Wkv"].reshape(D, G, 2, HD)
    wk, wv = kv[:, :, 0].reshape(D, G * HD), kv[:, :, 1].reshape(D, G * HD)
    gate = np.concatenate([a["L0_ffn_Wg"], a["L0_ffn_Sg"][None]])
    up = np.concatenate([a["L0_ffn_Wu"], a["L0_ffn_Su"][None]])
    down = np.concatenate([a["L0_ffn_Wd"], a["L0_ffn_Sd"][None]])
    gu = np.concatenate([gate.transpose(0, 2, 1), up.transpose(0, 2, 1)], axis=2)
    gu = gu.reshape(NE + 1, KD, P, 2 * FI).transpose(0, 2, 1, 3).reshape(NE + 1, P, GUC)
    dn = down.transpose(0, 2, 1).reshape(NE + 1, FK, P, D).transpose(0, 2, 1, 3).reshape(NE + 1, P, FK * D)
    laid = {
        "x": a["L0_attn_x"].reshape(NTOK, D),
        "wqk": by_rows(np.concatenate([a["L0_attn_Wq"], wk], axis=1)),
        "wvg": by_rows(np.concatenate([wv, a["L0_ffn_gate_w"].T], axis=1)),
        "wo": by_rows(a["L0_attn_Wo"]),
        "bo": a["L0_attn_bo"],
        "ebias": a["L0_ffn_bias"],
        "wexp": np.concatenate([gu, dn], axis=2),
    }
    laid = {name: np.ascontiguousarray(v) for name, v in laid.items()}
    nc = bacc.Bacc("TRN2", target_bir_lowering=False, num_devices=1)
    args = [nc.dram_tensor(name, v.shape, mybir.dt.from_np(v.dtype), kind="ExternalInput").ap() for name, v in laid.items()]
    out = nc.dram_tensor("out", (NTOK, D), F32, kind="ExternalOutput").ap()
    block_program(nc, *args, out)
    result = run_bass_kernel_spmd(nc, [laid], core_ids=[0])
    return result.results[0]["out"].reshape(B, T, D)
```

```python
from contextlib import ExitStack

import concourse.bass as bass
from concourse import mybir

F32 = mybir.dt.float32
F32R = mybir.dt.float32r
BF16 = mybir.dt.bfloat16
F16 = mybir.dt.float16
I32 = mybir.dt.int32
ALU = mybir.AluOpType
ACT = mybir.ActivationFunctionType
AX = mybir.AxisListType

P = 128
B, T, D = 4, 256, 512
NTOK = B * T
NT = NTOK // P
KD = D // P
H, G = 32, 8
HD = D // H
REP = H // G
QT = T // P
NE, TOPK, FI = 16, 4, 256
FK = FI // P
NSLOT = (TOPK * NTOK + (NE - TOPK) + NE * (P - 1)) // P
BESIDE = ((0, 1), (2,), (3,), (4, 5), (6,), (7, 8), (9,), (10, 11))
SPS = sum(len(s) for s in BESIDE)
assert B * SPS == NSLOT + 1 and SPS % 2 == 0
NCOL = 1 + NSLOT
WCOLS = KD * 2 * FI + FK * D
GUC = KD * 2 * FI
PARTS = (slice(0, GUC), slice(GUC, WCOLS))
HALVES = (slice(0, GUC // 2), slice(GUC // 2, GUC))
STEPS = HALVES + PARTS[1:]
VG = G * HD + NE
QROWS = 3 * HD
VCOL = 3 * HD + 1
QF = H * HD // P
SCALE = HD ** -0.5
BIG = 1.0e30
EPS = 1e-5


class Steps:

    def __init__(self, eng, sem):
        self.eng, self.sem, self.base, self.n = eng, sem, 0, 0

    def did(self, instruction):
        instruction.then_inc(self.sem, 1)
        self.n += 1

    def wait(self):
        self.eng.wait_ge(self.sem, self.base + self.n)


def block_program(nc, x, wqk, wvg, wo, bo, ebias, wexp, out):
    table = nc.dram_tensor("slot_table", [P, NCOL * 2], F32, kind="Internal").ap()
    xn_rows = nc.dram_tensor("xn_rows", [NTOK + P, D], F32, kind="Internal").ap()
    q_parts = nc.dram_tensor("q_parts", [QF * P, 2, T], F32, kind="Internal").ap()
    k_parts = nc.dram_tensor("k_parts", [P, 2, NTOK], F32, kind="Internal").ap()

    ctx = ExitStack()
    with ctx:
        def sb(name, shape, dt):
            return ctx.enter_context(nc.sbuf_tensor(name, shape, dt))

        def sem(name):
            return ctx.enter_context(nc.semaphore(name))

        xn = sb("xn", [P, NT, D], F32)
        xT = sb("xT", [P, KD, NTOK], F32)
        wraw = sb("wraw", [P, 2, WCOLS], F32)
        wsplit = sb("wsplit", [P, 2, 2, WCOLS], F32R)
        wqk_sb = sb("wqk_sb", [P, KD, (H + G) * HD], F32)
        wo_sb = sb("wo_sb", [P, KD, D], F32)
        bo_sb = sb("bo_sb", [P, D], F32)
        ebias_sb = sb("ebias_sb", [P, NE], F32)
        stage = sb("stage", [P, 2, QF, T], F32R)
        q_pack = sb("q_pack", [P, H // 2, T], F32R)
        k_pack = sb("k_pack", [P, B, T], F32R)
        v_pack = sb("v_pack", [P, NT, G, VCOL + 1], BF16)
        ident = sb("ident", [P, P], F32)
        ident_b = sb("ident_b", [P, P], BF16)
        mask_b = sb("mask_b", [P, P], BF16)
        before_b = sb("before_b", [P, P], BF16)
        ones_b = sb("ones_b", [P, P], BF16)
        ones_f = sb("ones_f", [P, NT * NE], F32)
        kcount = sb("kcount", [P, TOPK], F32)
        tile4 = sb("tile4", [P, NT], F32)
        lim = sb("lim", [P, NT - 1], F32)
        siota = sb("siota", [P, NCOL], F32)
        tab = sb("tab", [P, NCOL, 2], F32)
        gidx = sb("gidx", [P, 2], I32)
        sidx = sb("sidx", [P, 2], I32)
        gnone = sb("gnone", [P, 9], F32)
        xg = sb("xg", [P, 2, D], F32)
        xgT = sb("xgT", [P, 2, 2, KD, P], F32R)
        th = sb("th", [P, 2, FI], F32)
        zh = sb("zh", [P, FI], F32)
        zz = sb("zz", [P, 2, FI], F32)
        zT = sb("zT", [P, 2, 2, FK, P], F32R)
        ysb = sb("ysb", [P, 2, D], F32)
        xflat = xn[:, :, :].rearrange("p t d -> p (t d)")
        pexp = xflat[:, 0:3072].rearrange("p (b n) -> p b n", b=2)
        att = xflat[:, 3072:4096].rearrange("p (a d) -> p a d", a=QT)
        phi = sb("phi", [P, 2, 1536], F16)
        plo = sb("plo", [P, 2, 1536], F16)
        phi_f, plo_f = (t[:, :, :].rearrange("p a n -> p (a n)").bitcast(F32) for t in (phi, plo))
        vg_sb = phi_f[:, 0:NT * VG].rearrange("p (t n) -> p t n", t=NT)
        wvg_sb = plo_f[:, 0:KD * VG].rearrange("p (k n) -> p k n", k=KD)
        negm = sb("negm", [P, 2, QT, H // 2], F32)
        negmT = sb("negmT", [QT * H // 2, P], F32R)
        den = sb("den", [P, QT * REP], F32)
        csum = sb("csum", [P, QT * REP, HD], F32)
        ctxs = sb("ctxs", [P, QT, D], F32)
        base = ctxs
        ctxT = stage[:, 0, :, :].rearrange("p f t -> p (f t)").bitcast(F32).rearrange("p (a k n) -> p a k n", a=QT, k=KD)
        stats = sb("stats", [P, NT, 6], F32)
        mv = sb("mv", [P, NT, 2], F32)
        sm = sb("sm", [P, 7, NT], F32)
        rt = xflat[:, 0:14 * NT * NE].rearrange("p (c t e) -> p c t e", c=14, t=NT)
        oh = xflat[:, 2048:4096].rearrange("p (c t k e) -> p c t k e", c=4, t=NT, k=TOPK)
        vres = xflat[:, 2048:4096].rearrange("p (c t n) -> p c t n", c=2, t=NT)
        top8 = sb("top8", [P, NT, 8], F32)
        need = sb("need", [P, 6, NT], F32)
        mask16 = sb("mask16", [P, NT, NE], BF16)
        ecount = sb("ecount", [P, 6, NE], F32)
        sgt = sb("sgt", [P, NE, NT - 1], F32)
        scmp = xflat[:, 3072:3072 + NCOL * NE].rearrange("p (s e) -> p s e", e=NE)
        sexp = sb("sexp", [P, 2, NCOL], F32)
        sexp_i = sb("sexp_i", [P, 3, NCOL], I32)
        where = sb("where", [P, 3, NCOL], I32)
        dest_f = sb("dest_f", [P, NT, TOPK], F32)
        dest_i = sb("dest_i", [P, NT, TOPK], I32)
        tpos_i = sb("tpos_i", [P, 4, NT, TOPK], I32)
        pair = sb("pair", [P, NT, TOPK, 2], F32)

        psum = ctx.enter_context(nc.psum_tensor("psum", [P, 8, 512], F32))

        def bank(i, cols=512):
            return psum[:, i, 0:cols]

        def sems(names):
            return [sem(n) for n in names.split()]

        (const_ready, sqrt_in, sqrt_done, dve_step, pool_step, xn_ready, xnT_ps, xnT_sb, xn_stored, vg_ps, vg_done,
         rexp_done, mask_ready, ranks_ps, slots_known, pair_ready, table_zero, scattered, table_back,
         v_ready) = sems(
            "const_ready sqrt_in sqrt_done dve_step pool_step xn_ready xnT_ps xnT_sb xn_stored vg_ps vg_done "
            "rexp_done mask_ready ranks_ps slots_known pair_ready table_zero scattered table_back v_ready")
        (xt_ps, xt_high, xt_sb, gu_ps, th_done, z_done, zt_ps, zt_high, zt_sb, dn_ps, y_sb, shared_done,
         xs_high, xs_low, ws_high, ws_low, *w_ready_high_low) = sems(
            "xt_ps xt_high xt_sb gu_ps th_done z_done zt_ps zt_high zt_sb dn_ps y_sb shared_done "
            "xs_high xs_low ws_high ws_low gu_ready down_ready gu_high down_high gu_low down_low")
        w_ready, w_high, w_low = (w_ready_high_low[i:i + 2] for i in (0, 2, 4))
        (proj_ps, hi_done, lo_done, ones_set, max_ps, negm_done, nmT_ps, nmT_sb, nm_in, st_ps, exp_done, masked,
         hi16_done, lo16_done, pv_ps, csum_done, ctx_done, ct_ps, ct_sb, wo_ps, att_sb, att_out, k_out, stored) = sems(
            "proj_ps hi_done lo_done ones_set max_ps negm_done nmT_ps nmT_sb nm_in st_ps exp_done masked "
            "hi16_done lo16_done pv_ps csum_done ctx_done ct_ps ct_sb wo_ps att_sb att_out k_out stored")
        wvg_in, wqk_in, wo_in, small_in = sems("wvg_in wqk_in wo_in small_in")
        x_in = [sem(f"x_in{i}") for i in range(4)]
        we_in = [[sem(f"{part}_in{i}") for i in range(2)] for part in ("gu", "down")]
        base_in = [sem(f"base_in{i}") for i in range(2)]
        xg_in = [sem(f"xg_in{i}") for i in range(2)]
        y_out = [sem(f"y_out{i}") for i in range(2)]
        parts_out = [sem(f"parts_out{i}") for i in range(QF)]
        packed = [sem(f"packed{i}") for i in range(2)]

        def arrivals(e):
            return e // 2 + 1 + e % 2

        HALF_PACK = 6 * 16
        U1 = NT + 1
        GU, XT, DN, PV = 5, 6, 7, 4
        WO = (PV, 3)

        block = ctx.enter_context(nc.Block())

        def pack_half(eng, half, b):
            for row, (kpart, qpart) in enumerate(((0, 0), (1, 0), (0, 1))):
                base = 64 * half + HD * row
                eng.dma_start(k_pack[base:base + HD, :, :].rearrange("r c t -> r (c t)").bitcast(F32),
                              k_parts[bass.ds(2 * HD * b + half * HD, HD), kpart, :]).then_inc(packed[half], 16)
                eng.dma_start(q_pack[base:base + HD, :, :].bitcast(F32),
                              q_parts[half * T:(half + 1) * T, qpart, :].rearrange("(h r) t -> r h t", r=HD)
                              ).then_inc(packed[half], 16)

        @block.sync
        def _(sp):
            for i in range(4):
                sp.dma_start(xn[:, 2 * i:2 * i + 2, :],
                             x[2 * i * P:(2 * i + 2) * P, :].rearrange("(t p) d -> p t d", p=P)).then_inc(x_in[i], 16)
            sp.dma_start(wvg_sb[:, :, :], wvg).then_inc(wvg_in, 16)
            sp.dma_start(ebias_sb[:, :], ebias.rearrange("(a n) -> a n", a=1).broadcast_to([P, NE])).then_inc(small_in, 16)
            sp.dma_start(bo_sb[:, :], bo.rearrange("(a n) -> a n", a=1).broadcast_to([P, D])).then_inc(small_in, 16)
            sp.dma_start(wqk_sb[:, :, :], wqk).then_inc(wqk_in, 16)

            def load_base(t):
                sp.dma_start(base[:, t % 2, :], x[t * P:(t + 1) * P, :]).then_inc(base_in[t % 2], 16)

            for part, cols in enumerate(PARTS):
                sp.dma_start(wraw[:, 1, cols], wexp[NE, :, cols]).then_inc(we_in[part][1], 16)
            for t in range(NT):
                sp.wait_ge(xn_ready, t + 1)
                sp.dma_start(xn_rows[t * P:(t + 1) * P, :], xn[:, t, :]).then_inc(xn_stored, 16)
            load_base(0)
            load_base(1)
            for c in range(B):
                sp.wait_ge(lo_done, c + 1)
                sp.dma_start(k_parts[:, :, c * T:(c + 1) * T], stage[:, :, c, :].bitcast(F32)).then_inc(k_out, 16)
            for f in range(QF):
                sp.wait_ge(lo_done, B + f + 1)
                sp.dma_start(q_parts[f * P:(f + 1) * P], stage[:, :, f, :].bitcast(F32)).then_inc(parts_out[f], 16)
            for part, cols in enumerate(PARTS):
                sp.dma_start(wraw[:, 0, cols], wexp[0, :, cols]).then_inc(we_in[part][0], 16)
            sp.wait_ge(k_out, 16 * B)
            sp.wait_ge(ones_set, 1)
            for half in range(2):
                for f in (2 * half, 2 * half + 1):
                    sp.wait_ge(parts_out[f], 16)
                pack_half(sp, half, 0)
            sp.dma_start(wo_sb[:, :, :], wo).then_inc(wo_in, 16)
            for part in range(2):
                sp.wait_ge(we_in[part][0], 16)
                sp.sem_inc(w_ready[part], 1)
            sp.wait_ge(ws_low, len(STEPS))
            for part, cols in enumerate(PARTS):
                sp.dma_start(wraw[:, 1, cols], wexp[1, :, cols]).then_inc(we_in[part][1], 16)
            for t in range(NT):
                sp.wait_ge(shared_done, t + 1)
                sp.dma_start(out[t * P:(t + 1) * P, :], base[:, t % 2, :]).then_inc(stored, 16)
                if t + 2 < NT:
                    sp.wait_ge(stored, 16 * (t + 1))
                    load_base(t + 2)
                if t == NT - 3:
                    sp.wait_ge(scattered, 16 * NT * TOPK)
                    sp.dma_start(tab[:, :, :].rearrange("p s c -> p (s c)"), table).then_inc(table_back, 16)
            def announce(part, e):
                sp.wait_ge(we_in[part][e % 2], 16 * arrivals(e))
                sp.sem_inc(w_ready[part], 1)

            def load(part, e):
                sp.wait_ge(w_low[part], (2 - part) * (e - 1))
                sp.dma_start(wraw[:, e % 2, PARTS[part]], wexp[e, :, PARTS[part]]).then_inc(we_in[part][e % 2], 16)

            announce(0, 1)
            for e in range(2, NE):
                load(0, e)
                if e > 2:
                    announce(1, e - 2)
                announce(0, e)
                if e > 2:
                    load(1, e - 1)
            announce(1, NE - 2)
            load(1, NE - 1)
            announce(1, NE - 1)

        @block.gpsimd
        def _(pool):
            own = Steps(pool, pool_step)
            pool.sem_inc(exp_done, 1)
            own.did(nc.gpsimd.memset(ident[:, :], 0.0))
            own.wait()
            own.did(nc.gpsimd.affine_select(out=ident[:, :], in_=ident[:, :], compare_op=ALU.not_equal, fill=1.0, base=0,
                                            pattern=[[-1, P]], channel_multiplier=1))
            own.wait()
            pool.sem_inc(const_ready, 1)
            own.did(nc.gpsimd.memset(ident_b[:, :], 0.0))
            own.did(nc.gpsimd.memset(mask_b[:, :], 0.0))
            own.did(nc.gpsimd.memset(before_b[:, :], 1.0))
            own.did(nc.gpsimd.memset(tab[:, :, 1], 0.0))
            own.did(nc.gpsimd.iota(tab[:, :, 0].bitcast(I32), pattern=[[0, NCOL]], base=NTOK, channel_multiplier=1))
            own.did(nc.gpsimd.memset(ones_b[:, :], 1.0))
            own.did(nc.gpsimd.memset(ones_f[:, :], 1.0))
            own.wait()
            own.did(nc.gpsimd.affine_select(out=ident_b[:, :], in_=ident_b[:, :], compare_op=ALU.not_equal, fill=1.0,
                                            base=0, pattern=[[-1, P]], channel_multiplier=1))
            own.did(nc.gpsimd.affine_select(out=mask_b[:, :], in_=mask_b[:, :], compare_op=ALU.is_ge, fill=-BIG, base=0,
                                            pattern=[[-1, P]], channel_multiplier=1))
            own.did(nc.gpsimd.affine_select(out=before_b[:, :], in_=before_b[:, :], compare_op=ALU.is_gt, fill=0.0, base=0,
                                            pattern=[[1, P]], channel_multiplier=-1))
            for m, step, base in ((kcount, 1, 1), (tile4, TOPK, 0), (lim, P, P), (siota, 1, -1)):
                own.did(nc.gpsimd.iota(m[:, :], pattern=[[step, m.shape[1]]], base=base, channel_multiplier=0,
                                       allow_small_or_imprecise_dtypes=True))
            for k in range(TOPK):
                own.did(nc.gpsimd.iota(pair[:, :, k, 0].bitcast(I32), pattern=[[P, NT]], base=0, channel_multiplier=1))
            own.wait()
            pool.sem_inc(const_ready, 1)
            pool.dma_start(table, tab[:, :, :].rearrange("p s c -> p (s c)")).then_inc(table_zero, 16)
            pool.wait_ge(small_in, 32)
            half_rows = NTOK + P // 2
            pool.dma_start(out[NTOK:half_rows, :], bo_sb[0:P // 2, :]).then_inc(y_out[0], 16)
            pool.dma_start(out[half_rows:NTOK + P, :], bo_sb[P // 2:P, :]).then_inc(y_out[1], 16)
            pool.dma_start(xn_rows[NTOK:NTOK + P, :], bo_sb[:, :]).then_inc(att_out, 16)
            pool.wait_ge(table_zero, 16)
            pool.wait_ge(pair_ready, 1)
            for j in range(NT):
                for k in range(TOPK):
                    nc.gpsimd.indirect_dma_start(
                        out=table.rearrange("p (s c) -> (p s) c", c=2),
                        out_offset=bass.IndirectOffsetOnAxis(ap=tpos_i[:, 3, j, k:k + 1], axis=0),
                        in_=pair[:, j, k, :], in_offset=None).then_inc(scattered, 16)
            pool.wait_ge(table_back, 16)
            pool.wait_ge(xn_stored, 16 * NT)

            def carry(i):
                own.did(nc.gpsimd.tensor_tensor(gnone[:, i:i + 1], ones_f[:, 0:1], ones_f[:, 0:1], ALU.mult))

            def gather(s, par, free):
                if free is not None:
                    pool.wait_ge(xt_ps, free)
                own.did(nc.gpsimd.tensor_copy(gidx[:, par:par + 1], tab[:, bass.ds(s + 1, 1), 0].bitcast(I32)))
                own.wait()
                carry(par)
                nc.gpsimd.indirect_dma_start(
                    out=xg[:, par, :], out_offset=None, in_=xn_rows,
                    in_offset=bass.IndirectOffsetOnAxis(ap=gidx[:, par:par + 1], axis=0)).then_inc(xg_in[par], 16)

            def causal(b, g):
                pool.wait_ge(exp_done, G * b + g + 2)
                carry(2)
                first = pexp[:, g % 2, 0:1024].rearrange("p (r q) -> p r q", r=REP)[:, :, 0:P]
                second = pexp[:, g % 2, 1024:1536].rearrange("p (r q) -> p r q", r=REP)
                for block_ in (first, second):
                    nc.gpsimd.affine_select(out=block_, in_=block_, compare_op=ALU.is_ge, fill=0.0, base=0,
                                            pattern=[[0, REP], [1, P]], channel_multiplier=-1).then_inc(masked, 1)

            def add_rows(b, j):
                s, par = SPS * b + (j - 1), 1 - j % 2
                pool.wait_ge(y_sb, s + 3)
                carry(3)
                own.did(nc.gpsimd.tensor_copy(sidx[:, par:par + 1], tab[:, bass.ds(s + 1, 1), 0].bitcast(I32)))
                own.wait()
                pool.wait_ge(y_out[1 - par], 8 * SPS * b + 16 * ((j + 1) // 2 + 1))
                carry(4)
                if j == 0:
                    pool.wait_ge(att_out, 16 * b + 16)
                    carry(5)
                nc.gpsimd.indirect_dma_start(
                    out=out, out_offset=bass.IndirectOffsetOnAxis(ap=sidx[:, par:par + 1], axis=0),
                    in_=ysb[:, par, :], in_offset=None, compute_op=ALU.add).then_inc(y_out[par], 16)

            def down_low(place, number):
                pool.wait_ge(w_high[1], number)
                carry(8)
                nc.gpsimd.tensor_tensor(wsplit[:, place, 1, PARTS[1]], wraw[:, place, PARTS[1]],
                                        wsplit[:, place, 0, PARTS[1]].bitcast(F32), ALU.subtract).then_inc(w_low[1], 1)

            def down_low_of(s):
                number = pool.value_load(where[0:1, 2, bass.ds(s + 1, 1)], min_val=0, max_val=NE)
                with pool.If(number > 0):
                    place = pool.value_load(where[0:1, 0, bass.ds(s + 1, 1)], min_val=0, max_val=1)
                    down_low(bass.ds(place, 1), number)
                with pool.Else():
                    carry(8)
                    own.n -= 1
                pool.end_ifs()

            def add_attention(b):
                pool.wait_ge(att_sb, QT * b + (QT + 1))
                carry(6)
                pool.wait_ge(y_out[0], 8 * SPS * b + (8 * SPS + 16))
                carry(7)
                pool.dma_start(out[bass.ds(T * b, T), :].rearrange("(t p) d -> p t d", p=P), att[:, :, :],
                               accum_op=ALU.add).then_inc(att_out, 16)

            def sequence(b, last):
                for g in range(G):
                    causal(b, g)
                    for j in BESIDE[g]:
                        if not (last and j + 3 >= SPS - 1):
                            gather(SPS * b + (j + 3), 1 - j % 2, SPS * b + (j + 2))
                        if not (last and j == SPS - 1):
                            down_low_of(SPS * b + j)
                        add_rows(b, j)
                add_attention(b)

            gather(0, 0, None)
            gather(1, 1, None)
            gather(2, 0, 1)
            down_low(0, 1)
            pool.wait_ge(att_out, 16)
            pool.wait_ge(stored, 16 * NT)
            n0, each = own.n, G + 6 * SPS + 3
            with pool.Fori(0, B - 1) as b:
                own.base, own.n = n0 + each * b, 0
                sequence(b, False)
                assert own.n == each, own.n
            own.base, own.n = 0, n0 + (B - 1) * each
            sequence(B - 1, True)
            pool.wait_ge(att_out, 16 * B + 16)

        @block.scalar
        def _(act):
            S = nc.scalar.activation
            act.sem_inc(y_sb, 1)
            act.sem_inc(w_high[0], 1)
            act.wait_ge(sqrt_in, 1)
            S(sm[:, 1, :], sm[:, 0, :], ACT.Sqrt).then_inc(sqrt_done, 1)
            for t in range(NT):
                act.wait_ge(xnT_ps, t + 1)
                S(xT[:, :, t * P:(t + 1) * P], bank(t % 2).rearrange("p (k n) -> p k n", k=KD),
                  ACT.Copy).then_inc(xnT_sb, 1)
            for t in range(NT):
                act.wait_ge(vg_ps, t + 1)
                S(vg_sb[:, t, :], bank(2 + t % 2, VG), ACT.Copy).then_inc(vg_done, 1)
            act.wait_ge(vg_done, NT)
            act.wait_ge(xn_stored, 16 * NT)
            S(rt[:, 0, :, :], vg_sb[:, :, G * HD:VG], ACT.Exp, scale=-1.0).then_inc(rexp_done, 1)

            def high_part(n, f, src):
                act.wait_ge(proj_ps, n + 1)
                S(stage[:, 0, f, :], src, ACT.Copy).then_inc(hi_done, 1)

            for n in range(B + QF):
                if n == B:
                    act.wait_ge(we_in[0][1], 16)
                    act.wait_ge(we_in[1][1], 16)
                    for cols in STEPS:
                        S(wsplit[:, 0, 0, cols], wraw[:, 1, cols], ACT.Copy).then_inc(ws_high, 1)
                    act.wait_ge(k_out, 16 * B)
                high_part(n, n % QF, bank(n % 4, T))

            def tanh(n, par):
                act.wait_ge(gu_ps, n + 1 - (n >= U1) if isinstance(n, int) else n)
                if not isinstance(n, int) or n >= 2:
                    act.wait_ge(z_done, n - 1)
                S(th[:, par, :], bank(GU, FI), ACT.Tanh, scale=0.5).then_inc(th_done, 1)

            def z_high(n, par, source=DN):
                act.wait_ge(zt_ps, n + 1)
                S(zT[:, par, 0, :, :], bank(source, FI).rearrange("p (k n) -> p k n", k=FK),
                  ACT.Copy).then_inc(zt_high, 1)

            def x_high(s, par):
                act.wait_ge(xt_ps, s + 1)
                S(xgT[:, par, 0, :, :], bank(XT).rearrange("p (k n) -> p k n", k=KD), ACT.Copy).then_inc(xt_high, 1)

            def weights_high(place, number, cols, part):
                act.wait_ge(w_ready[part], number)
                S(wsplit[:, place, 0, cols], wraw[:, place, cols], ACT.Copy).then_inc(w_high[part], 1)

            def slot_parts(s, par, more):
                if not more:
                    z_high(s + (U1 - 1), par)
                    return
                number = act.value_load(where[0:1, 2, bass.ds(s + 2, 1)], min_val=0, max_val=NE)
                with act.If(number > 0):
                    place = act.value_load(where[0:1, 0, bass.ds(s + 2, 1)], min_val=0, max_val=1)
                    x_high(s + 1, par)
                    z_high(s + (U1 - 1), par)
                    weights_high(bass.ds(place, 1), number, HALVES[0], 0)
                    weights_high(bass.ds(place, 1), number, HALVES[1], 0)
                with act.Else():
                    x_high(s + 1, par)
                    z_high(s + (U1 - 1), par)
                act.end_ifs()

            def down_high(s):
                number = act.value_load(where[0:1, 2, bass.ds(s + 1, 1)], min_val=0, max_val=NE)
                with act.If(number > 0):
                    place = act.value_load(where[0:1, 0, bass.ds(s + 1, 1)], min_val=0, max_val=1)
                    weights_high(bass.ds(place, 1), number, PARTS[1], 1)
                act.end_ifs()

            def y_evac(b, j):
                s, par = SPS * b + (j - 1), 1 - j % 2
                act.wait_ge(dn_ps, s + (U1 + 1))
                act.wait_ge(y_out[par], 8 * SPS * b + 16 * (j // 2 + 1))
                S(ysb[:, par, :], bank(DN), ACT.Copy, scale=tab[:, bass.ds(s + 1, 1), 1]).then_inc(y_sb, 1)

            def xs_high_part(n):
                S(xgT[:, n % 2, 0, :, :], xT[:, :, n * P:(n + 1) * P], ACT.Copy).then_inc(xs_high, 1)

            xs_high_part(0)
            xs_high_part(1)
            for n in range(NT):
                if n:
                    z_high(n - 1, (n - 1) % 2, XT)
                tanh(n, n % 2)
                if n + 2 < NT:
                    xs_high_part(n + 2)
            z_high(NT - 1, 1, XT)

            def minus_maxima(idx, half):
                act.wait_ge(nmT_ps, idx + 1)
                S(negmT[:, :], psum[0:QT * H // 2, 3, 0:P], ACT.Copy).then_inc(nmT_sb, 1)
                act.wait_ge(nmT_sb, idx + 1)
                for qt in range(QT):
                    act.dma_start(q_pack[64 * half + QROWS:64 * half + QROWS + 1, :, qt * P:(qt + 1) * P].bitcast(F32),
                                  negmT[qt * H // 2:(qt + 1) * H // 2, :].bitcast(F32)).then_inc(nm_in, 16)

            minus_maxima(0, 0)
            for i, cols in enumerate(STEPS):
                if i == 2:
                    act.wait_ge(dn_ps, NT)
                weights_high(0, 1, cols, i // 2)
            x_high(0, 0)
            act.wait_ge(slots_known, 1)
            act.wait_ge(v_ready, 1)
            act.wait_ge(table_back, 16)

            def numerators(b, g):
                act.wait_ge(st_ps, G * b + g + 1)
                act.wait_ge(lo16_done, G * b + g + 1)
                S(pexp[:, g % 2, :], psum[:, 0:3, :].rearrange("p a n -> p (a n)"), ACT.Exp,
                  scale=SCALE).then_inc(exp_done, 1)

            def high16(b, g):
                act.wait_ge(masked, 2 * (G * b + g + 1))
                act.wait_ge(pv_ps, G * b + g + 1)
                S(phi[:, g % 2, :], pexp[:, g % 2, :], ACT.Copy).then_inc(hi16_done, 1)

            def context_evac(b):
                for qt in range(QT):
                    act.wait_ge(ct_ps, QT * b + qt + 1)
                    S(ctxT[:, qt, :, :], bank(qt).rearrange("p (k n) -> p k n", k=KD), ACT.Copy).then_inc(ct_sb, 1)

            def sequence(b, last):
                for g in range(G):
                    if g == 4 and not last:
                        for f in (0, 1):
                            act.wait_ge(parts_out[f], 16 * b + 32)
                        pack_half(act, 0, b + 1)
                    numerators(b, g)
                    if g < QF and not last:
                        high_part(QF * b + (B + QF + g), g, bank(3, T))
                    for j in BESIDE[g]:
                        s = SPS * b + j
                        slot_parts(s, 1 - j % 2, not (last and j + 1 >= SPS - 1))
                        if j == BESIDE[g][-1] and (g == 3 or g == 7 and not last):
                            minus_maxima(2 * b + (g // 4 + 1), 1 - g // 4)
                        if not (last and j == SPS - 1):
                            tanh(s + U1, j % 2)
                        if j == BESIDE[g][0]:
                            high16(b, g)
                        if j == BESIDE[g][0] and g < QF and not last:
                            act.wait_ge(lo_done, QF * b + (B + QF + g + 1))
                            act.dma_start(q_parts[g * P:(g + 1) * P], stage[:, :, g, :].bitcast(F32)).then_inc(parts_out[g], 16)
                        if not (last and j == SPS - 1):
                            down_high(s)
                        y_evac(b, j)
                if not last:
                    for f in range(QF):
                        act.wait_ge(parts_out[f], 16 * b + 32)
                context_evac(b)
                if not last:
                    pack_half(act, 1, b + 1)

            with act.Fori(0, B - 1) as b:
                sequence(b, False)
            sequence(B - 1, True)

        @block.vector
        def _(dve):
            own = Steps(dve, dve_step)
            V = nc.vector

            def op(ins):
                own.did(ins)
                own.wait()

            dve.sem_inc(lo16_done, 2)
            dve.sem_inc(csum_done, 1)
            dve.sem_inc(att_sb, 1)
            own.did(V.memset(k_pack[32:64, :, :].bitcast(F32), 1.0))
            own.did(V.memset(k_pack[96:128, :, :].bitcast(F32), 1.0))
            own.did(V.memset(v_pack[:, :, :, 3 * HD:VCOL + 1], 1.0))
            for t in range(NT):
                dve.wait_ge(x_in[t // 2], 16)
                own.did(V.bn_stats(stats[:, t, :], xn[:, t, :]))
            own.wait()
            for t in range(NT):
                own.did(V.bn_aggr(mv[:, t, :], stats[:, t, :]))
            own.wait()
            V.tensor_scalar(sm[:, 0, :], mv[:, :, 1], EPS, None, ALU.add).then_inc(sqrt_in, 1)
            dve.wait_ge(sqrt_done, 1)
            op(V.reciprocal(sm[:, 2, :], sm[:, 1, :]))
            op(V.tensor_tensor(sm[:, 3, :], sm[:, 2, :], sm[:, 2, :], ALU.mult))
            op(V.tensor_tensor(sm[:, 4, :], sm[:, 3, :], sm[:, 0, :], ALU.mult))
            op(V.tensor_scalar(sm[:, 5, :], sm[:, 4, :], -0.5, 1.5, ALU.mult, ALU.add))
            op(V.tensor_tensor(sm[:, 6, :], sm[:, 5, :], sm[:, 2, :], ALU.mult))
            for t in range(NT):
                V.tensor_scalar(xn[:, t, :], xn[:, t, :], mv[:, t, 0:1], sm[:, 6, t:t + 1], ALU.subtract,
                                ALU.mult).then_inc(xn_ready, 1)

            def over_experts(a):
                return a.rearrange("p (t a) -> p t a", a=1).broadcast_to([P, NT, NE])

            dve.wait_ge(const_ready, 2)
            dve.wait_ge(rexp_done, 1)
            dve.wait_ge(small_in, 32)
            op(V.tensor_scalar(rt[:, 1, :, :], rt[:, 0, :, :], 1.0, None, ALU.add))
            op(V.reciprocal(rt[:, 2, :, :], rt[:, 1, :, :]))
            score = rt[:, 3, :, :]
            op(V.tensor_tensor(score, rt[:, 2, :, :],
                               ebias_sb[:, :].rearrange("p (a e) -> p a e", a=1).broadcast_to([P, NT, NE]), ALU.add))
            for t in range(NT):
                own.did(V.max(top8[:, t, :], score[:, t, :]))
            own.wait()
            def low_part(n, f, src):
                dve.wait_ge(hi_done, n + 1)
                V.tensor_tensor(stage[:, 1, f, :], src, stage[:, 0, f, :].bitcast(F32), ALU.subtract).then_inc(lo_done, 1)

            low_part(0, 0, bank(0, T))
            fourth = top8[:, :, TOPK - 1:TOPK].broadcast_to([P, NT, NE])
            above, equal = rt[:, 4, :, :], rt[:, 5, :, :]
            own.did(V.tensor_tensor(above, score, fourth, ALU.is_gt))
            op(V.tensor_tensor(equal, score, fourth, ALU.is_equal))
            own.did(V.tensor_reduce(need[:, 0, :], above, AX.X, ALU.add))
            flat = lambda a: a.rearrange("p t e -> p (t e)")
            op(V.tensor_tensor_scan(flat(rt[:, 6, :, :]), ones_f[:, :], flat(equal), 0.0, ALU.mult, ALU.add))
            low_part(1, 1, bank(1, T))
            own.did(V.tensor_scalar(need[:, 1, :], need[:, 0, :], -1.0, float(TOPK), ALU.mult, ALU.add))
            op(V.tensor_tensor(need[:, 2, :], rt[:, 6, :, 0], equal[:, :, 0], ALU.subtract))
            op(V.tensor_tensor(need[:, 3, :], need[:, 1, :], need[:, 2, :], ALU.add))
            op(V.tensor_tensor(rt[:, 7, :, :], rt[:, 6, :, :], over_experts(need[:, 3, :]), ALU.is_le))
            op(V.tensor_tensor(rt[:, 8, :, :], rt[:, 7, :, :], equal, ALU.mult))
            chosen = rt[:, 9, :, :]
            op(V.tensor_tensor(chosen, rt[:, 8, :, :], above, ALU.add))
            V.tensor_copy(mask16[:, :, :], chosen).then_inc(mask_ready, 1)
            low_part(2, 2, bank(2, T))
            own.did(V.tensor_tensor_scan(flat(rt[:, 10, :, :]), ones_f[:, :], flat(chosen), 0.0, ALU.mult, ALU.add))
            op(V.tensor_tensor(rt[:, 11, :, :], chosen, score, ALU.mult))
            own.did(V.tensor_tensor(rt[:, 12, :, :], rt[:, 10, :, :], over_experts(tile4[:, :]), ALU.subtract))
            op(V.tensor_reduce(need[:, 4, :], rt[:, 11, :, :], AX.X, ALU.add))
            op(V.tensor_scalar(need[:, 4, :], need[:, 4, :], 1e-20, None, ALU.add))
            op(V.reciprocal(need[:, 5, :], need[:, 4, :]))
            op(V.tensor_tensor(rt[:, 13, :, :], rt[:, 11, :, :], over_experts(need[:, 5, :]), ALU.mult))

            low_part(3, 3, bank(3, T))

            def per_choice(a):
                return a.rearrange("p t (a e) -> p t a e", a=1).broadcast_to([P, NT, TOPK, NE])

            op(V.tensor_tensor(oh[:, 0], per_choice(rt[:, 12, :, :]),
                               kcount[:, :].rearrange("p (a k c) -> p a k c", a=1, c=1).broadcast_to([P, NT, TOPK, NE]),
                               ALU.is_equal))
            op(V.tensor_tensor(oh[:, 1], oh[:, 0], per_choice(chosen), ALU.mult))
            op(V.tensor_tensor(oh[:, 2], oh[:, 1], per_choice(rt[:, 13, :, :]), ALU.mult))
            op(V.tensor_reduce(pair[:, :, :, 1], oh[:, 2], AX.X, ALU.add))
            def ws_low_part(i):
                dve.wait_ge(ws_high, i + 1)
                V.tensor_tensor(wsplit[:, 0, 1, STEPS[i]], wraw[:, 1, STEPS[i]], wsplit[:, 0, 0, STEPS[i]].bitcast(F32),
                                ALU.subtract).then_inc(ws_low, 1)

            ws_low_part(0)
            low_part(B, 0, bank(0, T))
            low_part(B + 1, 1, bank(1, T))
            ws_low_part(1)
            low_part(B + 2, 2, bank(2, T))
            low_part(B + 3, 3, bank(3, T))

            def xs_low_part(n):
                dve.wait_ge(xs_high, n + 1)
                V.tensor_tensor(xgT[:, n % 2, 1, :, :], xT[:, :, n * P:(n + 1) * P],
                                xgT[:, n % 2, 0, :, :].bitcast(F32), ALU.subtract).then_inc(xs_low, 1)

            xs_low_part(0)
            ws_low_part(2)
            xs_low_part(1)
            dve.wait_ge(lo_done, 1)
            V.memset(negm[:, :, :, :], 0.0).then_inc(ones_set, 1)

            dve.wait_ge(ranks_ps, 2)
            op(V.tensor_copy(ecount[:, 0, :], bank(XT, NE)))
            by_limit = [P, NE, NT - 1]
            op(V.tensor_tensor(sgt[:, :, :], ecount[:, 0, :].rearrange("p (e a) -> p e a", a=1).broadcast_to(by_limit),
                               lim[:, :].rearrange("p (a m) -> p a m", a=1).broadcast_to(by_limit), ALU.is_gt))
            op(V.tensor_reduce(ecount[:, 1, :], sgt[:, :, :], AX.X, ALU.add))
            op(V.tensor_scalar(ecount[:, 2, :], ecount[:, 1, :], 1.0, None, ALU.add))
            op(V.tensor_tensor_scan(ecount[:, 3, :], ones_f[:, 0:NE], ecount[:, 2, :], 0.0, ALU.mult, ALU.add))
            op(V.tensor_tensor(ecount[:, 4, :], ecount[:, 3, :], ecount[:, 2, :], ALU.subtract))
            op(V.tensor_scalar(ecount[:, 5, :], ecount[:, 4, :], 1.0, float(P), ALU.add, ALU.mult))
            op(V.tensor_tensor(rt[:, 1, :, :], bank(PV, NT * NE).rearrange("p (t e) -> p t e", t=NT),
                               ecount[:, 5, :].rearrange("p (a e) -> p a e", a=1).broadcast_to([P, NT, NE]), ALU.add))
            op(V.tensor_tensor(oh[:, 3], oh[:, 1], per_choice(rt[:, 1, :, :]), ALU.mult))
            op(V.tensor_reduce(dest_f[:, :, :], oh[:, 3], AX.X, ALU.add))
            op(V.tensor_copy(dest_i[:, :, :], dest_f[:, :, :]))
            own.did(V.tensor_scalar(tpos_i[:, 0], dest_i[:, :, :], 7, None, ALU.arith_shift_right))
            op(V.tensor_scalar(tpos_i[:, 1], dest_i[:, :, :], P - 1, None, ALU.bitwise_and))
            op(V.tensor_scalar(tpos_i[:, 2], tpos_i[:, 1], float(NCOL), None, ALU.mult))
            V.tensor_tensor(tpos_i[:, 3], tpos_i[:, 2], tpos_i[:, 0], ALU.add).then_inc(pair_ready, 1)

            def slot_experts():
                by_slot = [P, NCOL, NE]
                op(V.tensor_tensor(scmp[:, :, :], siota[:, :].rearrange("p (s a) -> p s a", a=1).broadcast_to(by_slot),
                                   ecount[:, 3, :].rearrange("p (a e) -> p a e", a=1).broadcast_to(by_slot), ALU.is_ge))
                op(V.tensor_reduce(sexp[:, 0, :], scmp[:, :, :], AX.X, ALU.add))
                op(V.tensor_scalar(sexp[:, 1, :], sexp[:, 0, :], float(NE - 1), None, ALU.min))
                op(V.tensor_copy(sexp_i[:, 0, :], sexp[:, 1, :]))
                own.did(V.tensor_scalar(where[:, 0, :], sexp_i[:, 0, :], 1, None, ALU.bitwise_and))
                own.did(V.tensor_scalar(where[:, 1, :], sexp_i[:, 0, :], 1.0, None, ALU.add))
                own.did(V.memset(sexp_i[:, 1, 0:1], 0))
                op(V.tensor_tensor(sexp_i[:, 1, 1:NCOL], sexp_i[:, 0, 1:NCOL], sexp_i[:, 0, 0:NCOL - 1], ALU.subtract))
                V.tensor_tensor(where[:, 2, :], where[:, 1, :], sexp_i[:, 1, :], ALU.mult).then_inc(slots_known, 1)

            val = vg_sb[:, :, 0:G * HD].rearrange("p t (g d) -> p t g d", g=G)
            res = [vres[:, c].rearrange("p t (g d) -> p t g d", g=G) for c in range(2)]
            vp = [v_pack[:, :, :, c * HD:(c + 1) * HD] for c in range(3)]

            def split_value(c):
                if c < 2:
                    op(V.tensor_copy(vp[c], val if c == 0 else res[c - 1]))
                    op(V.tensor_tensor(res[c], val if c == 0 else res[c - 1], vp[c], ALU.subtract))
                else:
                    V.tensor_copy(vp[c], res[c - 1]).then_inc(v_ready, 1)

            def gated(n, par):
                dve.wait_ge(th_done, n + 1 - (n >= U1) if isinstance(n, int) else n)
                if not isinstance(n, int) or n:
                    dve.wait_ge(z_done, n)
                own.did(V.scalar_tensor_tensor(out=zh[:, :], in0=th[:, par, :], scalar=1.0, in1=bank(GU, FI),
                                               op0=ALU.add, op1=ALU.mult))
                own.wait()
                if not isinstance(n, int) or n >= 2:
                    dve.wait_ge(zt_ps, n - 1)
                V.scalar_tensor_tensor(out=zz[:, par, :], in0=zh[:, :], scalar=0.5, in1=psum[:, GU, FI:2 * FI],
                                       op0=ALU.mult, op1=ALU.mult).then_inc(z_done, 1)

            def shared_out(n):
                dve.wait_ge(dn_ps, n + 1)
                dve.wait_ge(base_in[n % 2], 16 * (n // 2 + 1))
                V.tensor_tensor(base[:, n % 2, :], base[:, n % 2, :], bank(DN), ALU.add).then_inc(shared_done, 1)

            def z_low(n, par, source=DN):
                dve.wait_ge(zt_high, n + 1)
                V.tensor_tensor(zT[:, par, 1, :, :], bank(source, FI).rearrange("p (k n) -> p k n", k=FK),
                                zT[:, par, 0, :, :].bitcast(F32), ALU.subtract).then_inc(zt_sb, 1)

            def maxima(m, g):
                for qt in range(QT):
                    dve.wait_ge(max_ps, QT * m + qt + 1)
                    s_ = psum[:, 2 * qt:2 * qt + 2, :].rearrange("p a (r n) -> p (a r) n", r=2)[:, :, 0:(qt + 1) * P]
                    V.tensor_reduce(negm[:, g // 4, qt, REP * (g % 4):REP * (g % 4) + REP], s_, AX.X, ALU.max,
                                    negate=True).then_inc(negm_done, 1)

            for n in range(NT):
                if n:
                    z_low(n - 1, (n - 1) % 2, XT)
                gated(n, n % 2)
                if n + 2 < NT:
                    xs_low_part(n + 2)
                if n:
                    shared_out(n - 1)
                if n == 0:
                    slot_experts()
                if n % 2:
                    maxima(n // 2, n // 2)
                elif n < 6:
                    split_value(n // 2)
            z_low(NT - 1, 1, XT)
            shared_out(NT - 1)
            dve.wait_ge(stored, 16 * NT)
            dve.wait_ge(zt_ps, NT)
            dve.wait_ge(z_done, NT)
            V.memset(zz[:, 1, :], 0.0).then_inc(z_done, 1)

            def x_low(s, par):
                dve.wait_ge(xt_high, s + 1)
                V.tensor_tensor(xgT[:, par, 1, :, :], bank(XT).rearrange("p (k n) -> p k n", k=KD),
                                xgT[:, par, 0, :, :].bitcast(F32), ALU.subtract).then_inc(xt_sb, 1)

            def gu_low(place, number, half):
                dve.wait_ge(w_high[0], 2 * number + half)
                V.tensor_tensor(wsplit[:, place, 1, HALVES[half]], wraw[:, place, HALVES[half]],
                                wsplit[:, place, 0, HALVES[half]].bitcast(F32), ALU.subtract).then_inc(w_low[0], 1)

            def slot_parts(s, par, more):
                if not more:
                    z_low(s + (U1 - 1), par)
                    return
                number = dve.value_load(where[0:1, 2, bass.ds(s + 2, 1)], min_val=0, max_val=NE)
                with dve.If(number > 0):
                    place = dve.value_load(where[0:1, 0, bass.ds(s + 2, 1)], min_val=0, max_val=1)
                    x_low(s + 1, par)
                    z_low(s + (U1 - 1), par)
                    gu_low(bass.ds(place, 1), number, 0)
                    gu_low(bass.ds(place, 1), number, 1)
                with dve.Else():
                    x_low(s + 1, par)
                    z_low(s + (U1 - 1), par)
                dve.end_ifs()

            def low16(b, g):
                dve.wait_ge(hi16_done, G * b + g + 1)
                V.tensor_tensor(plo[:, g % 2, :], pexp[:, g % 2, :], phi[:, g % 2, :], ALU.subtract).then_inc(lo16_done, 1)

            def context(b, g):
                i = G * b + g
                dve.wait_ge(pv_ps, i + 3)
                sums = bank(PV, QT * REP * VCOL).rearrange("p (c n) -> p c n", c=QT * REP)
                own.did(V.reciprocal(den[:, :], sums[:, :, VCOL - 1]))
                V.tensor_reduce(csum[:, :, :], sums[:, :, 0:3 * HD].rearrange("p c (j d) -> p c d j", j=3), AX.X,
                                ALU.add).then_inc(csum_done, 1)
                own.wait()
                dve.wait_ge(csum_done, i + 2)
                V.tensor_tensor(ctxs[:, :, g * REP * HD:(g + 1) * REP * HD].rearrange("p a (r d) -> p a r d", r=REP),
                                csum[:, :, :].rearrange("p (a r) d -> p a r d", a=QT),
                                den[:, :].rearrange("p (a r c) -> p a r c", a=QT, c=1).broadcast_to([P, QT, REP, HD]),
                                ALU.mult).then_inc(ctx_done, 1)
                dve.wait_ge(ctx_done, i + 1)

            def attention_out(b):
                for qt in range(QT):
                    dve.wait_ge(wo_ps, QT * b + qt + 1)
                    if qt == 0:
                        dve.wait_ge(att_out, 16 * b + 16)
                    V.tensor_tensor(att[:, qt, :], bank(WO[qt]), bo_sb[:, :], ALU.add).then_inc(att_sb, 1)

            def sequence(b, last):
                for g in range(G):
                    if g < QF and not last:
                        low_part(QF * b + (B + QF + g), g, bank(3, T))
                    for j in BESIDE[g]:
                        s = SPS * b + j
                        slot_parts(s, 1 - j % 2, not (last and j + 1 >= SPS - 1))
                        if not (last and j == SPS - 1):
                            gated(s + U1, j % 2)
                        if j == BESIDE[g][0] and not (last and g >= 4):
                            maxima(G * b + (g + 4), (g + 4) % G)
                        if j == BESIDE[g][0]:
                            if g:
                                context(b, g - 1)
                            low16(b, g)
                    if g == G - 1:
                        context(b, g)
                attention_out(b)

            gu_low(0, 1, 0)
            gu_low(0, 1, 1)
            x_low(0, 0)
            n3, each = own.n, G + SPS
            with dve.Fori(0, B - 1) as b:
                own.base, own.n = n3 + each * b, 0
                sequence(b, False)
                assert own.n == each
            own.base, own.n = 0, n3 + (B - 1) * each
            sequence(B - 1, True)

        @block.tensor
        def _(pe):
            MM, TR = nc.tensor.matmul, nc.tensor.transpose
            pe.sem_inc(pv_ps, 2)
            pe.wait_ge(const_ready, 1)
            for t in range(NT):
                pe.wait_ge(xn_ready, t + 1)
                if t >= 2:
                    pe.wait_ge(xnT_sb, t - 1)
                for k in range(KD):
                    last = TR(psum[:, t % 2, k * P:(k + 1) * P], xn[:, t, k * P:(k + 1) * P], ident[:, :])
                last.then_inc(xnT_ps, 1)
            pe.wait_ge(wvg_in, 16)
            for t in range(NT):
                pe.wait_ge(xnT_sb, t + 1)
                if t >= 2:
                    pe.wait_ge(vg_done, t - 1)
                for k in range(KD):
                    last = MM(bank(2 + t % 2, VG), xT[:, k, t * P:(t + 1) * P], wvg_sb[:, k, :], start=k == 0,
                              stop=k == KD - 1)
                last.then_inc(vg_ps, 1)

            def project(dst, first, col):
                for k in range(KD):
                    last = MM(dst, wqk_sb[:, k, col:col + P],
                              xT[:, k:k + 1, bass.ds(first, T)].rearrange("p a n -> p (a n)"), start=k == 0, stop=k == KD - 1)
                last.then_inc(proj_ps, 1)

            pe.wait_ge(wqk_in, 16)
            pe.wait_ge(vg_done, NT)
            for n in range(B + QF):
                if n >= 4:
                    pe.wait_ge(lo_done, n - 3)
                if n < B:
                    project(bank(n % 4, T), n * T, QF * P)
                else:
                    project(bank(n % 4, T), 0, (n - B) * P)

            pe.wait_ge(const_ready, 2)
            pe.wait_ge(mask_ready, 1)
            MM(bank(PV, NT * NE), before_b[:, :], mask16[:, :, :].rearrange("p t e -> p (t e)"), start=True, stop=False,
               skip_group_check=True)
            for i in range(NT - 1):
                last = MM(psum[:, PV, (i + 1) * NE:NT * NE].rearrange("p (t e) -> p t e", e=NE), ones_b[:, :],
                          mask16[:, i:i + 1, :].broadcast_to([P, NT - 1 - i, NE]), start=False,
                          stop=i == NT - 2, skip_group_check=True)
            last.then_inc(ranks_ps, 1)
            for i in range(NT):
                last = MM(bank(XT, NE), ones_b[:, :], mask16[:, i, :], start=i == 0, stop=i == NT - 1)
            last.then_inc(ranks_ps, 1)

            def split_weights(place, part, c):
                if isinstance(place, int):
                    return wsplit[:, place, part, c:c + 512]
                return wsplit[:, bass.ds(place, 1), part, c:c + 512].rearrange("p a n -> p (a n)")

            def split_product(dst, lhs, place, first_col, tiles):
                products = [(k, a, w) for k in range(tiles) for a, w in ((0, 0), (0, 1), (1, 0))]
                for m, (k, a, w) in enumerate(products):
                    c = first_col + k * 512
                    last = MM(dst, lhs(a, k), split_weights(place, w, c),
                              start=m == 0, stop=m == len(products) - 1)
                return last

            def gate_up(par, place):
                split_product(bank(GU), lambda a, k: xgT[:, par, a, k, :], place, 0, KD).then_inc(gu_ps, 1)

            def z_transpose(n, par, to=DN):
                pe.wait_ge(z_done, n + 1)
                for k in range(FK):
                    last = TR(psum[:, to, k * P:(k + 1) * P], zz[:, par, k * P:(k + 1) * P], ident[:, :])
                last.then_inc(zt_ps, 1)

            def down(n, par, place):
                pe.wait_ge(zt_sb, n + 1)
                split_product(bank(DN), lambda a, k: zT[:, par, a, k, :], place, GUC, FK).then_inc(dn_ps, 1)

            def scores_for_max(b, m, g, lo_count=None):
                lo = 64 * (g // 4)
                if lo_count is not None:
                    pe.wait_ge(lo_done, lo_count)
                for qt in range(QT):
                    for pr in range(2):
                        dst = 2 * qt + pr
                        for r in range(2):
                            MM(psum[:, dst, r * T:(r + 1) * T],
                               q_pack[lo:lo + QROWS, REP * (g % 4) + 2 * pr + r, qt * P:(qt + 1) * P],
                               k_pack[lo:lo + QROWS, g % 4, :], start=r == 0, stop=False, skip_group_check=True)
                        last = MM(psum[:, dst, :].rearrange("p (r n) -> p r n", r=2)[:, :, qt * P:(qt + 1) * P],
                                  ident_b[:, :], mask_b[:, :].rearrange("p (a n) -> p a n", a=1).broadcast_to([P, 2, P]),
                                  start=False, stop=True, skip_group_check=True)
                    last.then_inc(max_ps, 1)

            def maxima_transpose(steps, half):
                pe.wait_ge(negm_done, 2 * steps)
                TR(psum[0:QT * H // 2, 3, 0:P], negm[:, half, :, :].rearrange("p a h -> p (a h)"),
                   ident[:, :]).then_inc(nmT_ps, 1)

            pe.wait_ge(ws_low, 2)
            for n in range(NT):
                if n:
                    z_transpose(n - 1, (n - 1) % 2, XT)
                pe.wait_ge(xs_low, n + 1)
                gate_up(n % 2, 0)
                if n % 2:
                    if n == 1:
                        pe.wait_ge(lo_done, B + QF)
                        pe.wait_ge(packed[0], HALF_PACK)
                    else:
                        pe.wait_ge(negm_done, 2 * (n // 2))
                    scores_for_max(0, n // 2, n // 2)
                if n:
                    pe.wait_ge(ws_low, 3)
                    if n >= 2:
                        pe.wait_ge(shared_done, n - 1)
                    down(n - 1, (n - 1) % 2, 0)
            maxima_transpose(4, 0)
            z_transpose(NT - 1, 1, XT)
            pe.wait_ge(shared_done, NT - 1)
            down(NT - 1, 1, 0)

            def scores(b, g, max_steps):
                lo, h0 = 64 * (g // 4), REP * (g % 4)
                pe.wait_ge(exp_done, G * b + g + 1)
                pe.wait_ge(negm_done, 2 * max_steps)
                if g % 4 == 0:
                    pe.wait_ge(nm_in, 32 * (2 * b + g // 4 + 1))
                if g == 0:
                    pe.wait_ge(att_sb, QT * b + 1)
                rows = slice(lo, lo + QROWS + 1)
                for pr in range(2):
                    MM(psum[:, pr, :], k_pack[rows, g % 4, 0:P], q_pack[rows, h0 + 2 * pr:h0 + 2 * pr + 2, :],
                       start=True, stop=True)
                MM(psum[:, 2, :], k_pack[rows, g % 4, P:T], q_pack[rows, h0:h0 + REP, P:T],
                   start=True, stop=True).then_inc(st_ps, 1)

            def weighted(b, g):
                i = G * b + g
                pe.wait_ge(lo16_done, i + 3)
                pe.wait_ge(csum_done, i + 1)
                for qt in range(QT):
                    for r in range(REP):
                        c = (qt * REP + r) * VCOL
                        parts = [(p_, kt) for kt in range(qt + 1) for p_ in (phi, plo)]
                        for m, (p_, kt) in enumerate(parts):
                            col = r * T + qt * P if kt == 0 else 2 * 512 + r * P
                            last = MM(psum[:, PV, c:c + VCOL], p_[:, g % 2, col:col + P],
                                      v_pack[:, QT * (g % B) + kt, bass.ds(2 * b + g // B, 1), 0:VCOL]
                                      .rearrange("p a n -> p (a n)"),
                                      start=m == 0, stop=m == len(parts) - 1, skip_group_check=True)
                last.then_inc(pv_ps, 1)

            def output_projection(b, nm_count):
                pe.wait_ge(ctx_done, G * (b + 1))
                pe.wait_ge(exp_done, G * (b + 1) + 1)
                for qt in range(QT):
                    for k in range(KD):
                        last = TR(psum[:, qt, k * P:(k + 1) * P], ctxs[:, qt, k * P:(k + 1) * P], ident[:, :])
                    last.then_inc(ct_ps, 1)
                pe.wait_ge(nmT_sb, nm_count)
                for qt in range(QT):
                    pe.wait_ge(ct_sb, QT * b + qt + 1)
                    for k in range(KD):
                        last = MM(bank(WO[qt]), ctxT[:, qt, k, :], wo_sb[:, k, :], start=k == 0, stop=k == KD - 1)
                    last.then_inc(wo_ps, 1)


            def rows_transpose(s, par, count):
                pe.wait_ge(xg_in[par], count)
                if not isinstance(s, int) or s:
                    pe.wait_ge(xt_sb, s)
                for k in range(KD):
                    last = TR(psum[:, XT, k * P:(k + 1) * P], xg[:, par, k * P:(k + 1) * P], ident[:, :])
                last.then_inc(xt_ps, 1)

            pe.wait_ge(slots_known, 1)
            rows_transpose(0, 0, 16)
            pe.wait_ge(wo_in, 16)
            pe.wait_ge(v_ready, 1)
            pe.wait_ge(shared_done, NT)

            def sequence(b, last):
                s0 = SPS * b

                def expert_of(s):
                    return (pe.value_load(where[0:1, 0, bass.ds(s + 1, 1)], min_val=0, max_val=1),
                            pe.value_load(where[0:1, 1, bass.ds(s + 1, 1)], min_val=1, max_val=NE))

                prev = expert_of(s0 - 1)
                for g in range(G):
                    scores(b, g, G * b + (min(g + 4, G) if last else g + 4))
                    if g < QF and not last:
                        project(bank(3, T), T * (b + 1), g * P)
                    for j in BESIDE[g]:
                        s, first = s0 + j, j == BESIDE[g][0]
                        real = not (last and j == SPS - 1)
                        if real:
                            place, number = expert_of(s)
                        if not (last and j + 1 >= SPS - 1):
                            rows_transpose(s + 1, 1 - j % 2, 8 * SPS * b + 16 * ((j + 1) // 2 + 1))
                        pe.wait_ge(y_sb, s + 1)
                        z_transpose(s + (U1 - 1), 1 - j % 2)
                        if j == BESIDE[g][-1] and (g == 3 or g == 7 and not last):
                            maxima_transpose(G * b + (g + 5), 1 - g // 4)
                        if real:
                            pe.wait_ge(w_low[0], 2 * number)
                            pe.wait_ge(xt_sb, s + 1)
                            gate_up(j % 2, place)
                        if first and not (last and g >= 4):
                            pe.wait_ge(exp_done, G * b + g + 2)
                            half = 1 - g // 4
                            if g % 4 == 0:
                                pe.wait_ge(packed[half], HALF_PACK * (b + 2 - half))
                            scores_for_max(b, G * b + (g + 4), (g + 4) % G,
                                           QF * b + (B + QF + g + 1) if g < QF and not last else None)
                        pe.wait_ge(w_low[1], prev[1])
                        down(s + (U1 - 1), 1 - j % 2, prev[0])
                        if first:
                            if g:
                                weighted(b, g - 1)
                        elif g == G - 1:
                            weighted(b, g)
                        if real:
                            prev = place, number
                output_projection(b, 2 * b + (2 if last else 3))

            with pe.Fori(0, B - 1) as b:
                sequence(b, False)
            sequence(B - 1, True)


def kernel(**inputs):
    import concourse.bacc as bacc
    import numpy as np
    from concourse.bass_utils import run_bass_kernel_spmd

    a = {name: np.asarray(v) for name, v in inputs.items()}

    def by_rows(w):
        return w.reshape(-1, P, w.shape[-1]).transpose(1, 0, 2)

    kv = a["L0_attn_Wkv"].reshape(D, G, 2, HD)
    wk, wv = kv[:, :, 0].reshape(D, G * HD), kv[:, :, 1].reshape(D, G * HD)
    gate = np.concatenate([a["L0_ffn_Wg"], a["L0_ffn_Sg"][None]])
    up = np.concatenate([a["L0_ffn_Wu"], a["L0_ffn_Su"][None]])
    down = np.concatenate([a["L0_ffn_Wd"], a["L0_ffn_Sd"][None]])
    gu = np.concatenate([gate.transpose(0, 2, 1), up.transpose(0, 2, 1)], axis=2)
    gu = gu.reshape(NE + 1, KD, P, 2 * FI).transpose(0, 2, 1, 3).reshape(NE + 1, P, GUC)
    dn = down.transpose(0, 2, 1).reshape(NE + 1, FK, P, D).transpose(0, 2, 1, 3).reshape(NE + 1, P, FK * D)
    laid = {
        "x": a["L0_attn_x"].reshape(NTOK, D),
        "wqk": by_rows(np.concatenate([a["L0_attn_Wq"], wk], axis=1)),
        "wvg": by_rows(np.concatenate([wv, a["L0_ffn_gate_w"].T], axis=1)),
        "wo": by_rows(a["L0_attn_Wo"]),
        "bo": a["L0_attn_bo"],
        "ebias": a["L0_ffn_bias"],
        "wexp": np.concatenate([gu, dn], axis=2),
    }
    laid = {name: np.ascontiguousarray(v) for name, v in laid.items()}
    nc = bacc.Bacc("TRN2", target_bir_lowering=False, num_devices=1)
    args = [nc.dram_tensor(name, v.shape, mybir.dt.from_np(v.dtype), kind="ExternalInput").ap() for name, v in laid.items()]
    out = nc.dram_tensor("out", (NTOK + P, D), F32, kind="ExternalOutput").ap()
    block_program(nc, *args, out)
    result = run_bass_kernel_spmd(nc, [laid], core_ids=[0])
    return result.results[0]["out"][:NTOK].reshape(B, T, D)
```
